# Optimizing a Trainium2 kernel written in Bass

```python
import numpy as np
import jax
import jax.numpy as jnp

def _softmax(x, axis=-1):
    return jax.nn.softmax(x, axis=axis)

def _gelu(x):
    return jax.nn.gelu(x, approximate=True)

def _silu(x):
    return jax.nn.silu(x)

def _sigmoid(x):
    return jax.nn.sigmoid(x)

def _layernorm(x, axis=-1, eps=1e-05):
    m = jnp.mean(x, axis=axis, keepdims=True)
    v = jnp.var(x, axis=axis, keepdims=True)
    return (x - m) / jnp.sqrt(v + eps)

def _scatter_add(tgt, idx, src, axis=0):
    return tgt.at[idx].add(src)

def _segment_sum(src, seg, n):
    return jax.ops.segment_sum(src, seg, n)
kernel_name = 'mk_dlrm_tower_d1_rec_r8_ad3c55'

def setup_inputs(seed: int=0):
    np.random.seed(seed)
    _w = jnp.asarray

    def _rec_inputs():
        import jax
        import jax.numpy as jnp
        _tk = jax.random.key(seed)
        dense_ctx = jax.random.normal(jax.random.fold_in(_tk, 190), (2048, 16), jnp.float32)
        ids = jnp.stack([jax.random.randint(jax.random.fold_in(_tk, 200 + f), (2048,), 0, v, jnp.int32) for f, v in enumerate([125000, 1250, 1250, 1000, 12500, 1250, 1000, 125000, 12500, 1250, 12500, 125000, 125000, 12500, 12500, 1000, 125000, 125000, 12500, 125000, 12500, 1000, 125000, 12500, 1000, 1250, 12500, 1250, 125000, 12500, 1000, 12500, 1250, 1250, 1000, 12500, 125000, 1000, 1000])], axis=1)
        tbl_0 = 0.05 * jax.random.normal(jax.random.fold_in(_tk, 500 + 0), (125000, 16), jnp.float32)
        tbl_1 = 0.05 * jax.random.normal(jax.random.fold_in(_tk, 500 + 1), (1250, 16), jnp.float32)
        tbl_2 = 0.05 * jax.random.normal(jax.random.fold_in(_tk, 500 + 2), (1250, 16), jnp.float32)
        tbl_3 = 0.05 * jax.random.normal(jax.random.fold_in(_tk, 500 + 3), (1000, 16), jnp.float32)
        tbl_4 = 0.05 * jax.random.normal(jax.random.fold_in(_tk, 500 + 4), (12500, 16), jnp.float32)
        tbl_5 = 0.05 * jax.random.normal(jax.random.fold_in(_tk, 500 + 5), (1250, 16), jnp.float32)
        tbl_6 = 0.05 * jax.random.normal(jax.random.fold_in(_tk, 500 + 6), (1000, 16), jnp.float32)
        tbl_7 = 0.05 * jax.random.normal(jax.random.fold_in(_tk, 500 + 7), (125000, 16), jnp.float32)
        tbl_8 = 0.05 * jax.random.normal(jax.random.fold_in(_tk, 500 + 8), (12500, 16), jnp.float32)
        tbl_9 = 0.05 * jax.random.normal(jax.random.fold_in(_tk, 500 + 9), (1250, 16), jnp.float32)
        tbl_10 = 0.05 * jax.random.normal(jax.random.fold_in(_tk, 500 + 10), (12500, 16), jnp.float32)
        tbl_11 = 0.05 * jax.random.normal(jax.random.fold_in(_tk, 500 + 11), (125000, 16), jnp.float32)
        tbl_12 = 0.05 * jax.random.normal(jax.random.fold_in(_tk, 500 + 12), (125000, 16), jnp.float32)
        tbl_13 = 0.05 * jax.random.normal(jax.random.fold_in(_tk, 500 + 13), (12500, 16), jnp.float32)
        tbl_14 = 0.05 * jax.random.normal(jax.random.fold_in(_tk, 500 + 14), (12500, 16), jnp.float32)
        tbl_15 = 0.05 * jax.random.normal(jax.random.fold_in(_tk, 500 + 15), (1000, 16), jnp.float32)
        tbl_16 = 0.05 * jax.random.normal(jax.random.fold_in(_tk, 500 + 16), (125000, 16), jnp.float32)
        tbl_17 = 0.05 * jax.random.normal(jax.random.fold_in(_tk, 500 + 17), (125000, 16), jnp.float32)
        tbl_18 = 0.05 * jax.random.normal(jax.random.fold_in(_tk, 500 + 18), (12500, 16), jnp.float32)
        tbl_19 = 0.05 * jax.random.normal(jax.random.fold_in(_tk, 500 + 19), (125000, 16), jnp.float32)
        tbl_20 = 0.05 * jax.random.normal(jax.random.fold_in(_tk, 500 + 20), (12500, 16), jnp.float32)
        tbl_21 = 0.05 * jax.random.normal(jax.random.fold_in(_tk, 500 + 21), (1000, 16), jnp.float32)
        tbl_22 = 0.05 * jax.random.normal(jax.random.fold_in(_tk, 500 + 22), (125000, 16), jnp.float32)
        tbl_23 = 0.05 * jax.random.normal(jax.random.fold_in(_tk, 500 + 23), (12500, 16), jnp.float32)
        tbl_24 = 0.05 * jax.random.normal(jax.random.fold_in(_tk, 500 + 24), (1000, 16), jnp.float32)
        tbl_25 = 0.05 * jax.random.normal(jax.random.fold_in(_tk, 500 + 25), (1250, 16), jnp.float32)
        tbl_26 = 0.05 * jax.random.normal(jax.random.fold_in(_tk, 500 + 26), (12500, 16), jnp.float32)
        tbl_27 = 0.05 * jax.random.normal(jax.random.fold_in(_tk, 500 + 27), (1250, 16), jnp.float32)
        tbl_28 = 0.05 * jax.random.normal(jax.random.fold_in(_tk, 500 + 28), (125000, 16), jnp.float32)
        tbl_29 = 0.05 * jax.random.normal(jax.random.fold_in(_tk, 500 + 29), (12500, 16), jnp.float32)
        tbl_30 = 0.05 * jax.random.normal(jax.random.fold_in(_tk, 500 + 30), (1000, 16), jnp.float32)
        tbl_31 = 0.05 * jax.random.normal(jax.random.fold_in(_tk, 500 + 31), (12500, 16), jnp.float32)
        tbl_32 = 0.05 * jax.random.normal(jax.random.fold_in(_tk, 500 + 32), (1250, 16), jnp.float32)
        tbl_33 = 0.05 * jax.random.normal(jax.random.fold_in(_tk, 500 + 33), (1250, 16), jnp.float32)
        tbl_34 = 0.05 * jax.random.normal(jax.random.fold_in(_tk, 500 + 34), (1000, 16), jnp.float32)
        tbl_35 = 0.05 * jax.random.normal(jax.random.fold_in(_tk, 500 + 35), (12500, 16), jnp.float32)
        tbl_36 = 0.05 * jax.random.normal(jax.random.fold_in(_tk, 500 + 36), (125000, 16), jnp.float32)
        tbl_37 = 0.05 * jax.random.normal(jax.random.fold_in(_tk, 500 + 37), (1000, 16), jnp.float32)
        tbl_38 = 0.05 * jax.random.normal(jax.random.fold_in(_tk, 500 + 38), (1000, 16), jnp.float32)
        _rk = jax.random.fold_in(_tk, 7)
        W_top1 = 0.0606339 * jax.random.normal(jax.random.fold_in(_tk, 801), (272, 512), jnp.float32)
        W_top2 = 0.0441942 * jax.random.normal(jax.random.fold_in(_tk, 802), (512, 256), jnp.float32)
        W_top3 = 0.0625 * jax.random.normal(jax.random.fold_in(_tk, 803), (256, 1), jnp.float32)
        b_top1 = jnp.zeros((512,), jnp.float32)
        b_top2 = jnp.zeros((256,), jnp.float32)
        return (dense_ctx, ids, tbl_0, tbl_1, tbl_2, tbl_3, tbl_4, tbl_5, tbl_6, tbl_7, tbl_8, tbl_9, tbl_10, tbl_11, tbl_12, tbl_13, tbl_14, tbl_15, tbl_16, tbl_17, tbl_18, tbl_19, tbl_20, tbl_21, tbl_22, tbl_23, tbl_24, tbl_25, tbl_26, tbl_27, tbl_28, tbl_29, tbl_30, tbl_31, tbl_32, tbl_33, tbl_34, tbl_35, tbl_36, tbl_37, tbl_38, W_top1, b_top1, W_top2, b_top2, W_top3)
    dense_ctx, ids, tbl_0, tbl_1, tbl_2, tbl_3, tbl_4, tbl_5, tbl_6, tbl_7, tbl_8, tbl_9, tbl_10, tbl_11, tbl_12, tbl_13, tbl_14, tbl_15, tbl_16, tbl_17, tbl_18, tbl_19, tbl_20, tbl_21, tbl_22, tbl_23, tbl_24, tbl_25, tbl_26, tbl_27, tbl_28, tbl_29, tbl_30, tbl_31, tbl_32, tbl_33, tbl_34, tbl_35, tbl_36, tbl_37, tbl_38, W_top1, b_top1, W_top2, b_top2, W_top3 = _rec_inputs()

    def _L0_rec_setup():
        import jax, jax.numpy as jnp
        import numpy as np
        B, F0, D = (256, 39, 16)
        LAYER_SIZES = [128, 128, 128]
        key = jax.random.key(seed)
        ks = jax.random.split(key, 1 + 2 * len(LAYER_SIZES))
        inputs = jax.random.normal(ks[0], (B, F0, D), dtype=jnp.float32)
        out = {'inputs': inputs}
        field_nums = [F0]
        for i, size in enumerate(LAYER_SIZES):
            fk = field_nums[-1]
            fan_in = F0 * fk
            scale = np.sqrt(2.0 / (fan_in + size)).astype(np.float32)
            out[f'w{i}'] = jax.random.normal(ks[1 + 2 * i], (F0, fk, size), dtype=jnp.float32) * scale
            out[f'b{i}'] = jnp.zeros((size,), dtype=jnp.float32)
            field_nums.append(size // 2)
        return out
    _L0_rec_all = _L0_rec_setup()
    _L0_rec_in = {k: v for k, v in _L0_rec_all.items() if k in ('w0', 'w1', 'w2', 'b0', 'b1', 'b2')}
    del _L0_rec_all
    return {'dense_ctx': dense_ctx, 'ids': ids, 'tbl_0': tbl_0, 'tbl_1': tbl_1, 'tbl_2': tbl_2, 'tbl_3': tbl_3, 'tbl_4': tbl_4, 'tbl_5': tbl_5, 'tbl_6': tbl_6, 'tbl_7': tbl_7, 'tbl_8': tbl_8, 'tbl_9': tbl_9, 'tbl_10': tbl_10, 'tbl_11': tbl_11, 'tbl_12': tbl_12, 'tbl_13': tbl_13, 'tbl_14': tbl_14, 'tbl_15': tbl_15, 'tbl_16': tbl_16, 'tbl_17': tbl_17, 'tbl_18': tbl_18, 'tbl_19': tbl_19, 'tbl_20': tbl_20, 'tbl_21': tbl_21, 'tbl_22': tbl_22, 'tbl_23': tbl_23, 'tbl_24': tbl_24, 'tbl_25': tbl_25, 'tbl_26': tbl_26, 'tbl_27': tbl_27, 'tbl_28': tbl_28, 'tbl_29': tbl_29, 'tbl_30': tbl_30, 'tbl_31': tbl_31, 'tbl_32': tbl_32, 'tbl_33': tbl_33, 'tbl_34': tbl_34, 'tbl_35': tbl_35, 'tbl_36': tbl_36, 'tbl_37': tbl_37, 'tbl_38': tbl_38, 'W_top1': W_top1, 'b_top1': b_top1, 'W_top2': W_top2, 'b_top2': b_top2, 'W_top3': W_top3, 'L0_rec_w0': _L0_rec_in['w0'], 'L0_rec_w1': _L0_rec_in['w1'], 'L0_rec_w2': _L0_rec_in['w2'], 'L0_rec_b0': _L0_rec_in['b0'], 'L0_rec_b1': _L0_rec_in['b1'], 'L0_rec_b2': _L0_rec_in['b2']}

def reference(dense_ctx, ids, tbl_0, tbl_1, tbl_2, tbl_3, tbl_4, tbl_5, tbl_6, tbl_7, tbl_8, tbl_9, tbl_10, tbl_11, tbl_12, tbl_13, tbl_14, tbl_15, tbl_16, tbl_17, tbl_18, tbl_19, tbl_20, tbl_21, tbl_22, tbl_23, tbl_24, tbl_25, tbl_26, tbl_27, tbl_28, tbl_29, tbl_30, tbl_31, tbl_32, tbl_33, tbl_34, tbl_35, tbl_36, tbl_37, tbl_38, W_top1, b_top1, W_top2, b_top2, W_top3, L0_rec_w0, L0_rec_w1, L0_rec_w2, L0_rec_b0, L0_rec_b1, L0_rec_b2):
    import jax
    import jax.numpy as jnp

    def _L0_rec_ref(inputs, w0, w1, w2, b0, b1, b2):
        import jax, jax.numpy as jnp
        import numpy as np
        B, F0, D = (256, 39, 16)
        LAYER_SIZES = [128, 128, 128]
        x0 = inputs
        xk = inputs
        params = [(w0, b0), (w1, b1), (w2, b2)]
        n_layers = len(params)
        direct = []
        for idx, (W, b) in enumerate(params):
            z = jnp.einsum('bhd,bkd,hks->bsd', x0, xk, W) + b[None, :, None]
            z = jax.nn.relu(z)
            if idx != n_layers - 1:
                half = z.shape[1] // 2
                xk = z[:, :half, :]
                direct.append(z[:, half:, :])
            else:
                direct.append(z)
        logit = jnp.sum(jnp.concatenate(direct, axis=1), axis=-1)
        return logit
    e = jnp.stack([tbl_0[ids[:, 0]], tbl_1[ids[:, 1]], tbl_2[ids[:, 2]], tbl_3[ids[:, 3]], tbl_4[ids[:, 4]], tbl_5[ids[:, 5]], tbl_6[ids[:, 6]], tbl_7[ids[:, 7]], tbl_8[ids[:, 8]], tbl_9[ids[:, 9]], tbl_10[ids[:, 10]], tbl_11[ids[:, 11]], tbl_12[ids[:, 12]], tbl_13[ids[:, 13]], tbl_14[ids[:, 14]], tbl_15[ids[:, 15]], tbl_16[ids[:, 16]], tbl_17[ids[:, 17]], tbl_18[ids[:, 18]], tbl_19[ids[:, 19]], tbl_20[ids[:, 20]], tbl_21[ids[:, 21]], tbl_22[ids[:, 22]], tbl_23[ids[:, 23]], tbl_24[ids[:, 24]], tbl_25[ids[:, 25]], tbl_26[ids[:, 26]], tbl_27[ids[:, 27]], tbl_28[ids[:, 28]], tbl_29[ids[:, 29]], tbl_30[ids[:, 30]], tbl_31[ids[:, 31]], tbl_32[ids[:, 32]], tbl_33[ids[:, 33]], tbl_34[ids[:, 34]], tbl_35[ids[:, 35]], tbl_36[ids[:, 36]], tbl_37[ids[:, 37]], tbl_38[ids[:, 38]]], axis=1)
    z = _L0_rec_ref(e, L0_rec_w0, L0_rec_w1, L0_rec_w2, L0_rec_b0, L0_rec_b1, L0_rec_b2)
    z = z.reshape(z.shape[0], -1)
    h = jnp.concatenate([z, dense_ctx], axis=1)
    h = jnp.maximum(h @ W_top1 + b_top1, 0.0)
    h = jnp.maximum(h @ W_top2 + b_top2, 0.0)
    y = h @ W_top3
    return y

_drawn_inputs = setup_inputs


def setup_inputs(seed=0):
    import zlib

    import numpy as np

    out = dict(_drawn_inputs(seed))
    spreads = {'b_top1': (0.0, 2.0),
     'b_top2': (0.0, 2.0),
     'L0_rec_b0': (0.0, 0.345),
     'L0_rec_b1': (0.0, 0.517),
     'L0_rec_b2': (0.0, 0.8)}
    factors = {'tbl_0': 8.0,
     'tbl_1': 8.0,
     'tbl_2': 8.0,
     'tbl_3': 8.0,
     'tbl_4': 8.0,
     'tbl_5': 8.0,
     'tbl_6': 8.0,
     'tbl_7': 8.0,
     'tbl_8': 8.0,
     'tbl_9': 8.0,
     'tbl_10': 8.0,
     'tbl_11': 8.0,
     'tbl_12': 8.0,
     'tbl_13': 8.0,
     'tbl_14': 8.0,
     'tbl_15': 8.0,
     'tbl_16': 8.0,
     'tbl_17': 8.0,
     'tbl_18': 8.0,
     'tbl_19': 8.0,
     'tbl_20': 8.0,
     'tbl_21': 8.0,
     'tbl_22': 8.0,
     'tbl_23': 8.0,
     'tbl_24': 8.0,
     'tbl_25': 8.0,
     'tbl_26': 8.0,
     'tbl_27': 8.0,
     'tbl_28': 8.0,
     'tbl_29': 8.0,
     'tbl_30': 8.0,
     'tbl_31': 8.0,
     'tbl_32': 8.0,
     'tbl_33': 8.0,
     'tbl_34': 8.0,
     'tbl_35': 8.0,
     'tbl_36': 8.0,
     'tbl_37': 8.0,
     'tbl_38': 8.0,
     'L0_rec_w0': 8.0,
     'L0_rec_w1': 6.137,
     'L0_rec_w2': 4.692,
     'dense_ctx': 8.0}
    for name, (base, spread) in spreads.items():
        noise = np.random.default_rng([zlib.crc32(name.encode()), seed]).standard_normal(out[name].shape)
        drawn = base * np.exp(spread * noise) if base else spread * noise
        out[name] = jnp.asarray(drawn.astype(out[name].dtype))
    for name, factor in factors.items():
        out[name] = (out[name] * factor).astype(out[name].dtype)
    return out
```

```python
from contextlib import ExitStack

import concourse.bass as bass
from concourse import mybir

FP32 = mybir.dt.float32
FP32R = mybir.dt.float32r
I32 = mybir.dt.int32
ALU = mybir.AluOpType
ACT = mybir.ActivationFunctionType

B, F0, D = 2048, 39, 16
S = 128
HALF = S // 2
U1, U2, DENSE = 512, 256, 16
BT = B // 128
DQ = 4
SLOTS = BT * D // DQ
C = DQ * 128
HG, KG = 5, 4
NB0 = 7
STEPS = 20
PER_IT = 4 * STEPS
RING = 4
LAG = 3

CHUNKS = [(0, 0, 2, 2), (0, 2, 2, 2), (0, 4, 2, 2), (0, 6, 1, 1)]
for _layer in (1, 2):
    for _kg in range(KG):
        CHUNKS += [(_layer, _kg * HG, 3, 2), (_layer, _kg * HG + 3, 2, 1)]
LAST = {0: 3, 1: 11, 2: 19}
FIRST = {0: 0, 1: 4, 2: 12}
SPLIT_HG = (0, 1, 3)
FULL_HG = (2, 4)
MAX_SPLIT = 2

SUM_STEP = {0: LAST[0] + LAG + 1, 1: LAST[1] + LAG + 1, 2: LAST[2] + LAG + 1 - STEPS}
GATHERS = F0 // 3
SIDE_FIRST = 4
N_X = 1 + HG + 1


def pool_split(q, j):
    layer, _, _, ns = CHUNKS[j % STEPS]
    if layer == 0:
        return 1 if ns == 2 else 0
    if q == 3:
        return 1
    return 1 if ns == 1 or j % 4 == 0 else 0


def has_chunk(t):
    g, layer = t // STEPS, CHUNKS[t % STEPS][0]
    return t >= 0 and layer <= g < SLOTS + layer


def chunks(t):
    return sum(has_chunk(s) for s in range(t + 1))


def pool_subs(t):
    return sum(has_chunk(s) and pool_split(s // STEPS % 4, s % STEPS) > 0 for s in range(t + 1))


def dve_subs(t):
    return sum(has_chunk(s) and CHUNKS[s % STEPS][3] > pool_split(s // STEPS % 4, s % STEPS)
               for s in range(t + 1))


def column_of(t, layer):
    g, j = t // STEPS, t % STEPS
    if t < 0 or j != SUM_STEP[layer]:
        return None
    c = g - layer - (1 if layer == 2 else 0)
    return c if 0 <= c < SLOTS else None


def sums(t):
    return sum(column_of(s, layer) is not None for s in range(t + 1) for layer in range(3))


def later_sums(t):
    return sum((column_of(s, layer) or 0) % 4 > 0 for s in range(t + 1) for layer in range(3))


def lows(t):
    return sum(column_of(s, layer) is not None for s in range(t + 1) for layer in range(2))


def side_use(t):
    g, j = t // STEPS, t % STEPS
    if t < 0:
        return None
    if g + 1 < SLOTS and SIDE_FIRST <= j < SIDE_FIRST + N_X:
        return ("x", j - SIDE_FIRST)
    if g % 4 == 2 and 1 <= g // 4 <= BT and j in (13, 15, 17):
        return ("top", (j - 13) // 2)
    return None


def sides(t):
    return N_X + sum(side_use(s) is not None for s in range(t + 1))


TOP_DONE = 2 * STEPS + 17
N_LOADS = 5 + 4 + 6

_known = {}


def count(events, it, j):
    def at(n):
        key = (events, n, j)
        if key not in _known:
            _known[key] = events(PER_IT * n + j)
        return _known[key]
    if isinstance(it, int):
        return at(it)
    assert at(1) > 0
    each = at(2) - at(1)
    assert all(at(n) == at(1) + (n - 1) * each for n in range(2, BT - 1))
    return it * each + (at(1) - each)


def wait(engine, sem, value):
    if not isinstance(value, int) or value > 0:
        engine.wait_ge(sem, value)


def build(nc, ids, tables, dense_t, w0a, w0b, w1, w2, biases, wt1, wt1d, wt2, wt3, bt1, bt2,
          sel_in, ident_in, out):
    ctx = ExitStack()
    with ctx:
        def sb(name, shape, dt=FP32):
            return ctx.enter_context(nc.sbuf_tensor(name, shape, dt))

        def sem(name):
            return ctx.enter_context(nc.semaphore(name))

        ids_sb = sb("ids_sb", [128, F0], I32)
        emb = sb("emb", [128, F0 * D])
        emb_hl = sb("emb_hl", [128, 2, F0, D], FP32R)
        x_t = sb("x_t", [128, 2, C], FP32R)
        x_rep = sb("x_rep", [128, 4, HG, C])
        x_rep0 = sb("x_rep0", [128, 2, C])
        prod = sb("prod", [128, RING, 3, C])
        prod_h = sb("prod_h", [128, RING, MAX_SPLIT, C], FP32R)
        prod_l = sb("prod_l", [128, RING, MAX_SPLIT, C], FP32R)
        NS = len(SPLIT_HG)
        w0h = sb("w0h", [128, NB0, S], FP32R)
        w0l = sb("w0l", [128, NB0, S], FP32R)
        wh = {n: sb(f"w{n}h", [128, KG, NS, S], FP32R) for n in (1, 2)}
        wl = {n: sb(f"w{n}l", [128, KG, NS, S], FP32R) for n in (1, 2)}
        wf = {n: sb(f"w{n}f", [128, KG, HG - NS, S]) for n in (1, 2)}
        sel = sb("sel", [128, HG + 1 + NB0 + KG, 128], FP32R)
        SEL_X, SEL_ROT, SEL_K = 0, HG + 1, HG + 1 + NB0
        ident = sb("ident", [128, 128])
        bias = sb("bias", [128, 3])
        r = {n: sb(f"r{n}", [128, C]) for n in range(3)}
        xk = {n: sb(f"xk{n}", [128, 2, C], FP32R) for n in range(2)}
        half_sum = sb("half_sum", [128, 2, 128])
        dim_sum = sb("dim_sum", [128, 128])
        acc = {n: sb(f"acc{n}", [128, 128]) for n in range(3)}
        logits = {n: sb(f"logits{n}", [128, 128]) for n in range(3)}
        wt1_sb = sb("wt1_sb", [128, 3, U1])
        wt1d_sb = sb("wt1d_sb", [DENSE, U1])
        wt2_sb = sb("wt2_sb", [128, U1 // 128, U2])
        wt3_sb = sb("wt3_sb", [128, U2 // 128])
        bt1_sb = sb("bt1_sb", [128, U1 // 128])
        bt2_sb = sb("bt2_sb", [128, U2 // 128])
        dense_sb = sb("dense_sb", [DENSE, 128])
        h1 = sb("h1", [128, U1 // 128, 128])
        h2 = sb("h2", [128, U2 // 128, 128])
        y_sb = sb("y_sb", [1, 128])

        z = [ctx.enter_context(nc.psum_tensor(f"z{n}", [128, C], FP32)) for n in range(3)]
        rep = ctx.enter_context(nc.psum_tensor("rep", [128, 4, C], FP32))
        side = ctx.enter_context(nc.psum_tensor("side", [128, C], FP32))

        stage1 = prod[:, 0:2].rearrange("p r t c -> p (r t c)")[:, 0:KG * HG * S]
        stage2 = prod[:, 2:4].rearrange("p r t c -> p (r t c)")[:, 0:KG * HG * S]
        stage = {1: stage1.rearrange("p (k h s) -> p k h s", k=KG, h=HG),
                 2: stage2.rearrange("p (k h s) -> p k h s", k=KG, h=HG)}
        stage0 = x_rep[:, 3].rearrange("p t c -> p (t c)")
        stage0a = stage0[:, 0:NB0 * S]
        stage0b = stage0[:, NB0 * S:2 * NB0 * S]
        stage_sel = x_rep[:, 2].rearrange("p t c -> p (t c)")[:, 0:(SEL_K + KG) * 128]

        consts_in = sem("consts_in")
        weights_in = sem("weights_in")
        sel_ready = sem("sel_ready")
        w0_sum = sem("w0_sum")
        wh_ready = sem("wh_ready")
        wl_ready = sem("wl_ready")
        ids_in = sem("ids_in")
        gathered = sem("gathered")
        emb_h = sem("emb_h")
        emb_l = sem("emb_l")
        dense_in = sem("dense_in")
        selected = sem("selected")
        multiplied = sem("multiplied")
        rounded = sem("rounded")
        low_dve = sem("low_dve")
        low_pool = sem("low_pool")
        contracted = sem("contracted")
        side_ready = sem("side_ready")
        side_read = sem("side_read")
        layer_read = sem("layer_read")
        xk_low = sem("xk_low")
        summed = sem("summed")
        halved = sem("halved")
        quartered = sem("quartered")
        y_free = sem("y_free")

        block = ctx.enter_context(nc.Block())

        def each_iteration(engine, body):
            body(0, range(PER_IT))
            with engine.Fori(1, BT - 1) as it:
                body(it, range(PER_IT))
            body(BT - 1, range(PER_IT))
            body(BT, range(3 * STEPS))

        def absolute(it, j):
            return PER_IT * (it if isinstance(it, int) else 1) + j

        @block.sync
        def _(sp):
            sp.dma_start(ids_sb[:], ids[0:128, :]).then_inc(ids_in, 16)
            sp.dma_start(y_sb[:], dense_t[0:1, 0:128]).then_inc(y_free, 16)
            sp.dma_start(stage_sel, sel_in).then_inc(consts_in, 16)
            sp.dma_start(ident[:], ident_in).then_inc(consts_in, 16)
            loads = [(stage0a, w0a), (stage0b, w0b),
                     (stage1, w1.rearrange("p k h s -> p (k h s)")), (stage2, w2.rearrange("p k h s -> p (k h s)")),
                     (bias[:], biases)]
            for n, w in ((1, w1), (2, w2)):
                for i, hg in enumerate(FULL_HG):
                    loads.append((wf[n][:, :, i], w[:, :, hg]))
            loads += [(wt1_sb[:], wt1), (wt1d_sb[:], wt1d), (wt2_sb[:], wt2), (wt3_sb[:], wt3),
                      (bt1_sb[:], bt1), (bt2_sb[:], bt2)]
            for dst, src in loads:
                sp.dma_start(dst, src).then_inc(weights_in, 16)
            assert len(loads) == N_LOADS

            def next_ids(it):
                wait(sp, gathered, (it + 1) * (16 * F0))
                sp.dma_start(ids_sb[:], ids[bass.ds((it + 1) * 128, 128), :]).then_inc(ids_in, 16)

            def result(it):
                sp.wait_ge(side_read, count(sides, it, TOP_DONE - PER_IT))
                sp.dma_start(dense_sb[:], dense_t[:, bass.ds((it - 1) * 128, 128)]).then_inc(dense_in, 16)
                sp.wait_ge(side_read, count(sides, it, TOP_DONE))
                sp.dma_start(out[bass.ds(it - 1, 1), :], y_sb[:]).then_inc(y_free, 16)

            next_ids(0)
            with sp.Fori(1, BT - 1) as it:
                next_ids(it)
                result(it)
            result(BT - 1)
            result(BT)
            sp.wait_ge(y_free, 16 * (BT + 1))

        @block.gpsimd
        def _(pool):
            def lookup(f):
                nc.gpsimd.indirect_dma_start(
                    emb[:, f * D:(f + 1) * D], None, tables[f],
                    bass.IndirectOffsetOnAxis(ids_sb[:, f:f + 1], 0)).then_inc(gathered, 16)

            def low_part(it, j):
                t = absolute(it, j)
                q = t // STEPS % 4
                if not (has_chunk(t) and pool_split(q, j % STEPS)):
                    return
                n = CHUNKS[j % STEPS][3] - 1
                pool.wait_ge(rounded, count(chunks, it, j))
                nc.gpsimd.tensor_tensor(prod_l[:, j % RING, n], prod[:, j % RING, n],
                                        prod_h[:, j % RING, n].bitcast(FP32), ALU.subtract).then_inc(low_pool, 1)

            def add_up(it, j, layer):
                t = absolute(it, j)
                c = column_of(t, layer)
                if c is None:
                    return
                turn = count(sums, it, j)
                pool.wait_ge(layer_read, turn)
                wait(pool, summed, turn - 1)
                nc.gpsimd.tensor_tensor(half_sum[:].rearrange("p a b -> p (a b)"), r[layer][:, 0:256],
                                        r[layer][:, 256:512], ALU.add).then_inc(halved, 1)
                pool.wait_ge(halved, turn)
                if c % 4 == 0:
                    nc.gpsimd.tensor_tensor(acc[layer][:], half_sum[:, 0], half_sum[:, 1], ALU.add).then_inc(summed, 1)
                    return
                nc.gpsimd.tensor_tensor(dim_sum[:], half_sum[:, 0], half_sum[:, 1], ALU.add).then_inc(quartered, 1)
                pool.wait_ge(quartered, count(later_sums, it, j))
                if c % 4 < 3:
                    ins = nc.gpsimd.tensor_tensor(acc[layer][:], acc[layer][:], dim_sum[:], ALU.add)
                else:
                    wait(pool, side_read, count(sides, it, TOP_DONE - (0 if layer == 0 else PER_IT)))
                    ins = nc.gpsimd.tensor_tensor(logits[layer][:], acc[layer][:], dim_sum[:], ALU.add)
                ins.then_inc(summed, 1)

            def body(it, steps):
                for j in steps:
                    q, k = j // STEPS, j % STEPS
                    look_up = q < 3 and k < GATHERS and (not isinstance(it, int) or it < BT - 1)
                    if j == 0 and look_up:
                        pool.wait_ge(ids_in, (it + 2) * 16)
                        pool.wait_ge(emb_l, it + 1)
                    low_part(it, j)
                    if look_up:
                        lookup(q * GATHERS + k)
                    for layer in range(3):
                        add_up(it, j, layer)

            pool.wait_ge(ids_in, 16)
            for f in range(F0):
                lookup(f)
            each_iteration(pool, body)

        @block.scalar
        def _(act):
            def split_lookups(n):
                act.wait_ge(gathered, n * (16 * F0))
                nc.scalar.activation(emb_hl[:, 0].rearrange("p f d -> p (f d)"), emb[:], ACT.Copy).then_inc(emb_h, 1)

            def x_side(g, n, sides_done):
                act.wait_ge(side_ready, sides_done)
                if n == 0:
                    ins = nc.scalar.activation(x_t[0:2 * F0, g % 2], side[0:2 * F0, :], ACT.Copy)
                elif n <= HG:
                    ins = nc.scalar.activation(x_rep[:, g % 4, n - 1], side[:], ACT.Copy)
                else:
                    ins = nc.scalar.activation(x_rep0[:, g % 2], side[:], ACT.Copy)
                ins.then_inc(side_read, 1)

            def top_side(it, n, sides_done):
                act.wait_ge(side_ready, sides_done)
                if n == 0:
                    for m in range(U1 // 128):
                        ins = nc.scalar.activation(h1[:, m], side[:, m * 128:(m + 1) * 128], ACT.Relu,
                                                   bias=bt1_sb[:, m:m + 1])
                elif n == 1:
                    for m in range(U2 // 128):
                        ins = nc.scalar.activation(h2[:, m], side[:, m * 128:(m + 1) * 128], ACT.Relu,
                                                   bias=bt2_sb[:, m:m + 1])
                else:
                    act.wait_ge(y_free, it * 16)
                    ins = nc.scalar.activation(y_sb[:], side[0:1, 0:128], ACT.Copy)
                ins.then_inc(side_read, 1)

            def read_layer(it, j, layer):
                t = absolute(it, j)
                c = column_of(t, layer)
                if c is None:
                    return
                act.wait_ge(contracted, count(chunks, it, j - LAG - 1))
                wait(act, summed, count(sums, it, j - STEPS))
                if layer < 2:
                    wait(act, xk_low, count(lows, it, j - STEPS))
                ins = nc.scalar.activation(r[layer][:], z[layer][:], ACT.Relu, bias=bias[:, layer:layer + 1])
                if layer < 2:
                    p = slice(HALF, S) if layer == 0 else slice(0, HALF)
                    ins = nc.scalar.activation(xk[layer][p, c % 2], z[layer][p, :], ACT.Relu,
                                               bias=bias[p, layer:layer + 1])
                ins.then_inc(layer_read, 1)

            def body(it, steps):
                for j in steps:
                    t = absolute(it, j)
                    g = t // STEPS
                    if j == 3 * STEPS + 1 and (not isinstance(it, int) or it < BT - 1):
                        split_lookups(it + 2)
                    for layer in range(3):
                        read_layer(it, j, layer)
                    use = side_use(t)
                    if use and use[0] == "x":
                        x_side(g + 1, use[1], count(sides, it, j))
                    elif use:
                        top_side(it, use[1], count(sides, it, j))
                    if has_chunk(t):
                        ns = CHUNKS[j % STEPS][3]
                        act.wait_ge(multiplied, count(chunks, it, j))
                        nc.scalar.activation(prod_h[:, j % RING, 0:ns], prod[:, j % RING, 0:ns],
                                             ACT.Copy).then_inc(rounded, 1)

            act.wait_ge(w0_sum, 1)
            nc.scalar.activation(w0h[:].rearrange("p t s -> p (t s)"), stage0a, ACT.Copy).then_inc(wh_ready, 1)
            act.wait_ge(weights_in, 16 * N_LOADS)
            for n in (1, 2):
                for i, hg in enumerate(SPLIT_HG):
                    ins = nc.scalar.activation(wh[n][:, :, i], stage[n][:, :, hg], ACT.Copy)
                ins.then_inc(wh_ready, 1)
            split_lookups(1)
            for n in range(N_X):
                x_side(0, n, n + 1)
            each_iteration(act, body)

        @block.vector
        def _(dve):
            def split_lookups(n):
                dve.wait_ge(emb_h, n)
                nc.vector.tensor_tensor(emb_hl[:, 1].rearrange("p f d -> p (f d)"), emb[:],
                                        emb_hl[:, 0].rearrange("p f d -> p (f d)").bitcast(FP32),
                                        ALU.subtract).then_inc(emb_l, 1)

            def multiply(it, j):
                t = absolute(it, j)
                if not has_chunk(t):
                    return
                g, (layer, first, n, _) = t // STEPS, CHUNKS[j % STEPS]
                dst = prod[:, j % RING, 0:n]
                if layer == 0 and first == 0:
                    dve.wait_ge(side_read, count(sides, it, j - j % STEPS - 1))
                if layer == 0:
                    bank = first % 4
                    a = x_rep0[:, g % 2].unsqueeze(1).to_broadcast([128, n, C])
                    b = rep[:, bank:bank + n]
                else:
                    kg, hg = first // HG, first % HG
                    a = x_rep[:, (g - layer) % 4, hg:hg + n]
                    b = rep[:, kg].unsqueeze(1).to_broadcast([128, n, C])
                wait(dve, contracted, count(chunks, it, j - RING))
                dve.wait_ge(selected, count(chunks, it, j))
                nc.vector.tensor_tensor(dst, a, b, ALU.mult).then_inc(multiplied, 1)

            def low_part(it, j):
                t = absolute(it, j)
                if not has_chunk(t):
                    return
                ns = CHUNKS[j % STEPS][3]
                n = ns - pool_split(t // STEPS % 4, j % STEPS)
                if n == 0:
                    return
                dve.wait_ge(rounded, count(chunks, it, j))
                nc.vector.tensor_tensor(prod_l[:, j % RING, 0:n], prod[:, j % RING, 0:n],
                                        prod_h[:, j % RING, 0:n].bitcast(FP32), ALU.subtract).then_inc(low_dve, 1)

            def xk_low_part(it, j, layer):
                t = absolute(it, j)
                c = column_of(t, layer)
                if c is None:
                    return
                hi, lo = (slice(HALF, S), slice(0, HALF)) if layer == 0 else (slice(0, HALF), slice(HALF, S))
                dve.wait_ge(layer_read, count(sums, it, j))
                nc.vector.tensor_tensor(xk[layer][lo, c % 2], r[layer][hi], xk[layer][hi, c % 2].bitcast(FP32),
                                        ALU.subtract).then_inc(xk_low, 1)

            def body(it, steps):
                for j in steps:
                    multiply(it, j)
                    low_part(it, j - 1)
                    for layer in range(2):
                        xk_low_part(it, j, layer)
                    if j == 3 * STEPS + 2 and (not isinstance(it, int) or it < BT - 1):
                        split_lookups(it + 2)

            dve.wait_ge(consts_in, 32)
            nc.vector.tensor_copy(sel[:].rearrange("p t s -> p (t s)"), stage_sel).then_inc(sel_ready, 1)
            dve.wait_ge(weights_in, 16 * N_LOADS)
            nc.vector.tensor_tensor(stage0a, stage0a, stage0b, ALU.add).then_inc(w0_sum, 1)
            dve.wait_ge(w0_sum, 1)
            dve.wait_ge(wh_ready, 1)
            nc.vector.tensor_tensor(w0l[:].rearrange("p t s -> p (t s)"), stage0a,
                                    w0h[:].rearrange("p t s -> p (t s)").bitcast(FP32),
                                    ALU.subtract).then_inc(wl_ready, 1)
            for n in (1, 2):
                dve.wait_ge(wh_ready, n + 1)
                for i, hg in enumerate(SPLIT_HG):
                    ins = nc.vector.tensor_tensor(wl[n][:, :, i], stage[n][:, :, hg], wh[n][:, :, i].bitcast(FP32),
                                                  ALU.subtract)
                ins.then_inc(wl_ready, 1)
            split_lookups(1)
            dve.wait_ge(wl_ready, 3)
            each_iteration(dve, body)

        @block.tensor
        def _(pe):
            def x_side(g, n, sides_done):
                pe.wait_ge(side_read, sides_done - 1)
                if n == 0:
                    for i in range(DQ):
                        d = g % 4 * DQ + i
                        ins = nc.tensor.transpose(side[0:2 * F0, i * 128:(i + 1) * 128],
                                                  emb_hl[:, :, :, d].rearrange("p a f -> p (a f)").bitcast(FP32),
                                                  ident[:])
                else:
                    ins = nc.tensor.matmul(side[:], sel[0:2 * F0, SEL_X + n - 1], x_t[0:2 * F0, g % 2],
                                           start=True, stop=True)
                ins.then_inc(side_ready, 1)

            def top_side(it, n, sides_done):
                pe.wait_ge(side_read, sides_done - 1)
                if n == 0:
                    pe.wait_ge(dense_in, it * 16)
                    pe.wait_ge(summed, count(sums, it, 2 * STEPS + 12))
                    for m in range(U1 // 128):
                        o, cols = side[:, m * 128:(m + 1) * 128], slice(m * 128, (m + 1) * 128)
                        for n in range(3):
                            nc.tensor.matmul(o, wt1_sb[:, n, cols], logits[n][:], start=(n == 0), stop=False)
                        ins = nc.tensor.matmul(o, wt1d_sb[:, cols], dense_sb[:], start=False, stop=True)
                elif n == 1:
                    for m in range(U2 // 128):
                        for k in range(U1 // 128):
                            ins = nc.tensor.matmul(side[:, m * 128:(m + 1) * 128],
                                                   wt2_sb[:, k, m * 128:(m + 1) * 128], h1[:, k],
                                                   start=(k == 0), stop=(k == U1 // 128 - 1))
                else:
                    for k in range(U2 // 128):
                        ins = nc.tensor.matmul(side[0:1, 0:128], wt3_sb[:, k:k + 1], h2[:, k],
                                               start=(k == 0), stop=(k == U2 // 128 - 1))
                ins.then_inc(side_ready, 1)

            def select(it, j):
                t = absolute(it, j)
                if not has_chunk(t):
                    return
                g, (layer, first, n, _) = t // STEPS, CHUNKS[j % STEPS]
                if layer == 0:
                    if first == 0:
                        pe.wait_ge(side_read, count(sides, it, j - 1))
                    wait(pe, multiplied, count(chunks, it, j - 2))
                    for i in range(n):
                        ins = nc.tensor.matmul(rep[:, (first + i) % 4], sel[0:2 * F0, SEL_ROT + first + i],
                                               x_t[0:2 * F0, g % 2], start=True, stop=True)
                    ins.then_inc(selected, 1)
                elif first % HG == 0:
                    kg = first // HG
                    if kg == 0:
                        pe.wait_ge(xk_low, count(lows, it, j - j % STEPS - 1))
                    wait(pe, multiplied, count(chunks, it, j - 2))
                    nc.tensor.matmul(rep[:, kg], sel[:, SEL_K + kg], xk[layer - 1][:, (g - layer) % 2],
                                     start=True, stop=True).then_inc(selected, 2)

            def contract(it, j):
                t = absolute(it, j)
                if not has_chunk(t):
                    return
                layer, first, n, ns = CHUNKS[j % STEPS]
                k, place = j % STEPS, j % RING
                begin, end = k == FIRST[layer], k == LAST[layer]
                acc_z = z[layer][:]
                if begin:
                    wait(pe, layer_read, count(sums, it, j - k + SUM_STEP[layer] - (0 if layer == 2 else STEPS)))
                pe.wait_ge(multiplied, count(chunks, it, j))
                kg, hg = first // HG, first % HG
                for i in range(ns, n):
                    nc.tensor.matmul(acc_z, wf[layer][:, kg, FULL_HG.index(hg + i)], prod[:, place, i],
                                     start=begin and i == ns, stop=False)
                begin = begin and n == ns
                pe.wait_ge(rounded, count(chunks, it, j))
                if layer == 0:
                    w_high = [w0h[:, first + i] for i in range(ns)]
                    w_low = [w0l[:, first + i] for i in range(ns)]
                else:
                    w_high = [wh[layer][:, kg, SPLIT_HG.index(hg + i)] for i in range(ns)]
                    w_low = [wl[layer][:, kg, SPLIT_HG.index(hg + i)] for i in range(ns)]
                for i in range(ns):
                    nc.tensor.matmul(acc_z, w_high[i], prod_h[:, place, i], start=begin and i == 0, stop=False)
                    nc.tensor.matmul(acc_z, w_low[i], prod_h[:, place, i], start=False, stop=False)
                np_ = pool_split(t // STEPS % 4, k)
                if ns > np_:
                    pe.wait_ge(low_dve, count(dve_subs, it, j))
                for i in range(ns):
                    if np_ and i == ns - 1:
                        pe.wait_ge(low_pool, count(pool_subs, it, j))
                    ins = nc.tensor.matmul(acc_z, w_high[i], prod_l[:, place, i], start=False,
                                           stop=end and i == ns - 1)
                ins.then_inc(contracted, 1)

            def body(it, steps):
                for j in steps:
                    t = absolute(it, j)
                    select(it, j)
                    use = side_use(t)
                    if use and use[0] == "x":
                        if j == 3 * STEPS + SIDE_FIRST:
                            pe.wait_ge(emb_l, it + 2)
                        x_side(t // STEPS + 1, use[1], count(sides, it, j))
                    elif use:
                        top_side(it, use[1], count(sides, it, j))
                    contract(it, j - LAG)

            pe.wait_ge(consts_in, 32)
            pe.wait_ge(sel_ready, 1)
            pe.wait_ge(emb_l, 1)
            for n in range(N_X):
                if n == 0:
                    for i in range(DQ):
                        ins = nc.tensor.transpose(side[0:2 * F0, i * 128:(i + 1) * 128],
                                                  emb_hl[:, :, :, i].rearrange("p a f -> p (a f)").bitcast(FP32),
                                                  ident[:])
                    ins.then_inc(side_ready, 1)
                else:
                    x_side(0, n, n + 1)
            pe.wait_ge(weights_in, 16 * N_LOADS)
            pe.wait_ge(wl_ready, 3)
            each_iteration(pe, body)


def kernel(**inputs):
    import numpy as np
    import concourse.bacc as bacc
    from concourse.bass_utils import run_bass_kernel_spmd

    def a(name):
        return np.asarray(inputs[name])

    order0 = np.concatenate([np.arange(HALF, S), np.arange(0, HALF)])
    w0 = a("L0_rec_w0")[:, :, order0]
    w0a = np.zeros((128, NB0, S), w0.dtype)
    w0b = np.zeros((128, NB0, S), w0.dtype)
    n_sel = HG + 1 + NB0 + KG
    sel = np.zeros((128, n_sel, 128), np.float32)
    for tile in range(NB0):
        for jj in range(3):
            delta = 3 * tile + jj
            for h in range(F0):
                k, p = (h + delta) % F0, jj * F0 + h
                if delta <= F0 // 2:
                    w0a[p, tile] = w0[h, k]
                    if delta:
                        w0b[p, tile] = w0[k, h]
                sel[[k, F0 + k], HG + 1 + tile, p] = 1
                sel[[h, F0 + h], HG, p] = 1
    w12 = []
    for name in ("L0_rec_w1", "L0_rec_w2"):
        w = a(name)
        padded = np.zeros((HG * 8, HALF, S), w.dtype)
        padded[:F0] = w
        w12.append(padded.reshape(HG, 8, KG, 16, S).transpose(3, 1, 2, 0, 4).reshape(128, KG, HG, S))
    for p in range(128):
        for hg in range(HG):
            h = 8 * hg + p % 8
            if h < F0:
                sel[[h, F0 + h], hg, p] = 1
        for kg in range(KG):
            k = 16 * kg + p // 8
            sel[[k, HALF + k], HG + 1 + NB0 + kg, p] = 1

    wt1 = a("W_top1")
    wt1_layers = np.zeros((128, 3, U1), wt1.dtype)
    wt1_layers[:HALF, 0] = wt1[:HALF]
    wt1_layers[HALF:, 1] = wt1[HALF:S]
    wt1_layers[:, 2] = wt1[S:2 * S]
    arrays = {
        "ids": a("ids"),
        "dense_t": a("dense_ctx").T,
        "w0a": w0a.reshape(128, -1), "w0b": w0b.reshape(128, -1), "w1": w12[0], "w2": w12[1],
        "biases": np.stack([a("L0_rec_b0")[order0], a("L0_rec_b1"), a("L0_rec_b2")], axis=1),
        "wt1": wt1_layers,
        "wt1d": wt1[2 * S:],
        "wt2": a("W_top2").reshape(U1 // 128, 128, U2).transpose(1, 0, 2),
        "wt3": a("W_top3")[:, 0].reshape(U2 // 128, 128).T,
        "bt1": a("b_top1").reshape(U1 // 128, 128).T,
        "bt2": a("b_top2").reshape(U2 // 128, 128).T,
        "sel": sel.reshape(128, -1),
        "ident": np.eye(128, dtype=np.float32),
    }
    arrays.update({f"tbl_{f}": a(f"tbl_{f}") for f in range(F0)})
    arrays = {k: np.ascontiguousarray(v) for k, v in arrays.items()}

    nc = bacc.Bacc("TRN2", target_bir_lowering=False, num_devices=1)
    t = {k: nc.dram_tensor(f"in_{k}", v.shape, mybir.dt.from_np(v.dtype), kind="ExternalInput").ap()
         for k, v in arrays.items()}
    out = nc.dram_tensor("out", (BT, 128), FP32, kind="ExternalOutput").ap()
    build(nc, t["ids"], [t[f"tbl_{f}"] for f in range(F0)], t["dense_t"], t["w0a"], t["w0b"], t["w1"], t["w2"],
          t["biases"], t["wt1"], t["wt1d"], t["wt2"], t["wt3"], t["bt1"], t["bt2"], t["sel"], t["ident"], out)
    r = run_bass_kernel_spmd(nc, [{f"in_{k}": v for k, v in arrays.items()}], core_ids=[0])
    return r.results[0]["out"].reshape(B, 1)
```

```python
from contextlib import ExitStack

import concourse.bass as bass
from concourse import mybir

FP32 = mybir.dt.float32
FP32R = mybir.dt.float32r
I32 = mybir.dt.int32
ALU = mybir.AluOpType
ACT = mybir.ActivationFunctionType

B, F0, D = 2048, 39, 16
S = 128
HALF = S // 2
U1, U2, DENSE = 512, 256, 16
BT = B // 128
DQ = 4
SLOTS = BT * D // DQ
C = DQ * 128
HG, KG = 5, 4
NB0 = 7
STEPS = 20
PER_IT = 4 * STEPS
RING = 5
LEAD = 4
COPY_AHEAD = 2

MORE_SPLIT = ((2, 1),)
SPLIT0, FULL0 = (0, 2, 4, 6), (1, 3, 5)
SPLIT = {n: [(kg, hg) for kg in range(KG) for hg in (0, 1, 3) + ((4,) if (n, kg) in MORE_SPLIT else ())] for n in (1, 2)}
FULL = {n: [(kg, hg) for kg in range(KG) for hg in range(HG) if (kg, hg) not in SPLIT[n]] for n in (1, 2)}
MAX_SPLIT = 2
POOL_RESTS = (6, 10, 14, 18)
CHUNKS = [(0, 0, 2, 1), (0, 2, 2, 1), (0, 4, 2, 1), (0, 6, 1, 1)]
for _layer in (1, 2):
    for _kg in range(KG):
        for _hg, _n in ((0, 3), (3, 2)):
            _split = sum((_kg, hg) in SPLIT[_layer] for hg in range(_hg, _hg + _n))
            CHUNKS.append((_layer, _kg * HG + _hg, _n, _split))
LAST = {0: 3, 1: 11, 2: 19}
FIRST = {0: 0, 1: 4, 2: 12}
SUM_STEP = {0: LAST[0] + RING + 1, 1: LAST[1] + RING + 1, 2: LAST[2] + RING + 1 - STEPS}
PERIOD_START = -(STEPS - 2)
LOOKUP_END = 59
TOP_STEPS = (11, 15, 19)
TOP_DONE = 2 * STEPS + TOP_STEPS[2]
X_STEP = 0
ROWS0 = 3 * F0
X_ROWS = F0 + 3 * NB0


def pool_split(j):
    return 0 if j % STEPS in POOL_RESTS else 1


def has_chunk(t):
    g, layer = t // STEPS, CHUNKS[t % STEPS][0]
    return t >= 0 and layer <= g < SLOTS + layer


def chunks(t):
    return sum(has_chunk(s) for s in range(t + 1))


def replica(s):
    return has_chunk(s) and CHUNKS[s % STEPS][0] > 0 and CHUNKS[s % STEPS][1] % HG == 0


def replicas(t):
    return sum(replica(s) for s in range(t + 1))


def kg_replicas(t, kg):
    return sum(replica(s) and CHUNKS[s % STEPS][1] // HG == kg for s in range(t + 1))


replicas_of = [lambda t, kg=kg: kg_replicas(t, kg) for kg in range(KG)]


def pool_subs(t):
    return sum(has_chunk(s) and pool_split(s) > 0 for s in range(t + 1))


def dve_subs(t):
    return sum(has_chunk(s) and CHUNKS[s % STEPS][3] > pool_split(s)
               for s in range(t + 1))


def column_of(t, layer):
    g, j = t // STEPS, t % STEPS
    if t < 0 or j != SUM_STEP[layer]:
        return None
    c = g - layer - (1 if layer == 2 else 0)
    return c if 0 <= c < SLOTS else None


def sums(t):
    return sum(column_of(s, layer) is not None for s in range(t + 1) for layer in range(3))


def later_sums(t):
    return sum((column_of(s, layer) or 0) % 4 > 0 for s in range(t + 1) for layer in range(3))


def side_use(t):
    g, j = t // STEPS, t % STEPS
    if t < 0:
        return None
    if g + 1 < SLOTS and j == X_STEP:
        return "x"
    if g % 4 == 2 and 1 <= g // 4 <= BT and j in TOP_STEPS:
        return TOP_STEPS.index(j)
    return None


def sides(t):
    return 1 + sum(side_use(s) is not None for s in range(t + 1))


N_LOADS = 5 + len(FULL[1]) + len(FULL[2]) + 5

_known = {}


def count(events, it, j):
    def at(n):
        key = (events, n, j)
        if key not in _known:
            _known[key] = events(PER_IT * n + j)
        return _known[key]
    if isinstance(it, int):
        return at(it)
    assert at(1) > 0
    each = at(2) - at(1)
    assert all(at(n) == at(1) + (n - 1) * each for n in range(2, BT - 1))
    return it * each + (at(1) - each)


def wait(engine, sem, value):
    if not isinstance(value, int) or value > 0:
        engine.wait_ge(sem, value)


def build(nc, ids, tables, dense_t, w0a, w0b, w1, w2, biases, wt1, wt2, wt3, bt1, bt2,
          ident_dram, out):
    ctx = ExitStack()
    with ctx:
        def sb(name, shape, dt=FP32):
            return ctx.enter_context(nc.sbuf_tensor(name, shape, dt))

        def sem(name):
            return ctx.enter_context(nc.semaphore(name))

        ids_sb = sb("ids_sb", [128, F0], I32)
        emb = sb("emb", [128, F0 * D])
        emb_now = sb("emb_now", [128, 2, F0, D])
        x_t = sb("x_t", [2 * F0, C])
        x_rep = sb("x_rep", [128, 4, HG, C])
        x_rep0 = sb("x_rep0", [128, C])
        x_rot = sb("x_rot", [128, NB0, C])
        prod = sb("prod", [128, RING, 3, C])
        prod_h = sb("prod_h", [128, RING, MAX_SPLIT, C], FP32R)
        prod_l = sb("prod_l", [128, RING, MAX_SPLIT, C], FP32R)
        w0h = sb("w0h", [128, len(SPLIT0), S], FP32R)
        w0l = sb("w0l", [128, len(SPLIT0), S], FP32R)
        w0f = sb("w0f", [128, len(FULL0), S])
        wh = {n: sb(f"w{n}h", [128, len(SPLIT[n]), S], FP32R) for n in (1, 2)}
        wl = {n: sb(f"w{n}l", [128, len(SPLIT[n]), S], FP32R) for n in (1, 2)}
        wf = {n: sb(f"w{n}f", [128, len(FULL[n]), S]) for n in (1, 2)}
        ident = sb("ident", [128, 128])
        bias = sb("bias", [128, 3])
        r = {n: sb(f"r{n}", [128, C]) for n in range(3)}
        xk_rep = sb("xk_rep", [128, KG, C])
        half_sum = sb("half_sum", [128, 2, 128])
        dim_sum = sb("dim_sum", [128, 128])
        acc = {n: sb(f"acc{n}", [128, 128]) for n in range(3)}
        logits = {n: sb(f"logits{n}", [128, 128]) for n in range(3)}
        wt1_sb = sb("wt1_sb", [128, 3, U1])
        wt2_sb = sb("wt2_sb", [128, U1 // 128, U2])
        wt3_sb = sb("wt3_sb", [128, U2 // 128])
        bt1_sb = sb("bt1_sb", [128, U1 // 128])
        bt2_sb = sb("bt2_sb", [128, U2 // 128])
        h1 = sb("h1", [128, U1 // 128, 128])
        h2 = sb("h2", [128, U2 // 128, 128])
        y_sb = sb("y_sb", [1, 128])

        z = [ctx.enter_context(nc.psum_tensor(f"z{n}", [128, C], FP32)) for n in range(3)]
        rep = ctx.enter_context(nc.psum_tensor("rep", [128, 4, C], FP32))
        side = ctx.enter_context(nc.psum_tensor("side", [128, C], FP32))

        stage1 = prod[:, 0:2].rearrange("p r t c -> p (r t c)")[:, 0:KG * HG * S]
        stage2 = prod[:, 2:4].rearrange("p r t c -> p (r t c)")[:, 0:KG * HG * S]
        stage = {1: stage1.rearrange("p (k h s) -> p k h s", k=KG, h=HG),
                 2: stage2.rearrange("p (k h s) -> p k h s", k=KG, h=HG)}
        stage0 = x_rep[:, 3].rearrange("p t c -> p (t c)")
        stage0a = stage0[:, 0:NB0 * S].rearrange("p (t s) -> p t s", s=S)
        stage0b = stage0[:, NB0 * S:2 * NB0 * S].rearrange("p (t s) -> p t s", s=S)
        scratch = [nc.dram_tensor(f"scratch{i}", (X_ROWS, C), FP32, kind="Internal").ap() for i in range(2)]
        scratch_k = {n: nc.dram_tensor(f"scratch_k{n}", (HALF, C), FP32, kind="Internal").ap() for n in range(2)}

        ident_in = sem("ident_in")
        weights_in = sem("weights_in")
        w0_sum = sem("w0_sum")
        wh_ready = sem("wh_ready")
        wl_ready = sem("wl_ready")
        ids_in = sem("ids_in")
        gathered = sem("gathered")
        emb_moved = sem("emb_moved")
        x_out = sem("x_out")
        rot_in = [sem(f"rot_in{i}") for i in range(FIRST[1])]
        rep_in = sem("rep_in")
        pads = sem("pads")
        dense_in = sem("dense_in")
        copied = sem("copied")
        multiplied = sem("multiplied")
        rounded = sem("rounded")
        low_dve = sem("low_dve")
        low_pool = sem("low_pool")
        contracted = sem("contracted")
        side_ready = sem("side_ready")
        side_read = sem("side_read")
        layer_read = sem("layer_read")
        xk_out = {n: sem(f"xk_out{n}") for n in range(2)}
        xk_in = [sem(f"xk_in{kg}") for kg in range(KG)]
        summed = sem("summed")
        halved = sem("halved")
        quartered = sem("quartered")
        y_free = sem("y_free")

        block = ctx.enter_context(nc.Block())

        def each_iteration(engine, body):
            body(0, range(PER_IT))
            with engine.Fori(1, BT - 1) as it:
                body(it, range(PER_IT))
            body(BT - 1, range(PER_IT))
            body(BT, range(3 * STEPS + LEAD))

        def absolute(it, j):
            return PER_IT * (it if isinstance(it, int) else 1) + j

        @block.sync
        def _(sp):
            def values(*counts):
                return [c if isinstance(c, int) else sp.snap(c) for c in counts]

            def x_to_scratch(it, q):
                sp.wait_ge(side_read, count(sides, it, q * STEPS + X_STEP))
                sp.dma_start(scratch[(q + 1) % 2], x_t[0:X_ROWS]).then_inc(x_out, 16)

            def x_replicas(it, q):
                x = scratch[(q + 1) % 2]
                sp.wait_ge(x_out, (it * 4 + (q + 2)) * 16)
                sp.dma_start(x_rep0[0:ROWS0], x[0:F0].unsqueeze(1).to_broadcast([F0, 3, C])).then_inc(rot_in[0], 16)
                for i, (_, first, n, _) in enumerate(CHUNKS[:FIRST[1]]):
                    for t in range(first, first + n):
                        rows = x[3 * t:3 * t + F0]
                        window = bass.AP(tensor=rows.tensor, offset=rows.offset, ap=[[C, F0], [C, 3], [1, C]])
                        sp.dma_start(x_rot[0:ROWS0, t], window).then_inc(rot_in[i], 16)

            def x_replicas_12(it, q):
                x = scratch[(q + 1) % 2]
                for hg in range(HG):
                    rows = x[8 * hg:8 * hg + 8].unsqueeze(0).to_broadcast([16, 8, C])
                    sp.dma_start(x_rep[:, (q + 1) % 4, hg], rows).then_inc(rep_in, 16)

            def columns_before(it, q, behind):
                n = it * 4 + (q - behind)
                return None if isinstance(it, int) and not 0 <= n < SLOTS else n

            def xk_to_scratch(it, q, layer):
                if columns_before(it, q, layer) is None:
                    return
                other = q * STEPS + FIRST[2] if layer == 0 else (q + 1) * STEPS + FIRST[1]
                wait(sp, copied, count(replicas, it, other))
                if not replica(absolute(it, other)):
                    sp.wait_ge(layer_read, count(sums, it, q * STEPS + SUM_STEP[layer]))
                half = slice(HALF, S) if layer == 0 else slice(0, HALF)
                sp.dma_start(scratch_k[layer], r[layer][half]).then_inc(xk_out[layer], 16)

            def xk_replica(it, q, layer, kg):
                n = columns_before(it, q, layer + 1)
                if n is None:
                    return
                if kg == 0:
                    sp.wait_ge(xk_out[layer], n * 16 + 16)
                else:
                    before = FIRST[1] if layer == 1 else FIRST[2] - STEPS
                    wait(sp, copied, count(replicas, it, q * STEPS + before + 2 * kg))
                rows = scratch_k[layer][16 * kg:16 * kg + 16].unsqueeze(1).to_broadcast([16, 8, C])
                sp.dma_start(xk_rep[:, kg], rows).then_inc(xk_in[kg], 16)

            def slot(it, q, x=True):
                xk_to_scratch(it, q - 1, 1)
                if x:
                    x_to_scratch(it, q)
                xk_replica(it, q, 1, 0)
                xk_replica(it, q, 1, 1)
                if x:
                    x_replicas(it, q)
                xk_replica(it, q, 1, 2)
                xk_replica(it, q, 1, 3)
                xk_to_scratch(it, q, 0)
                if x:
                    x_replicas_12(it, q)
                for kg in range(KG):
                    xk_replica(it, q + 1, 0, kg)

            sp.dma_start(ids_sb[:], ids[0:128, :]).then_inc(ids_in, 16)
            sp.dma_start(y_sb[:], dense_t[0:1, 0:128]).then_inc(y_free, 16)
            sp.dma_start(ident[:], ident_dram).then_inc(ident_in, 16)
            loads = [(stage0a, w0a), (stage0b, w0b),
                     (stage1, w1.rearrange("p k h s -> p (k h s)")), (stage2, w2.rearrange("p k h s -> p (k h s)")),
                     (bias[:], biases)]
            for n, w in ((1, w1), (2, w2)):
                for i, (kg, hg) in enumerate(FULL[n]):
                    loads.append((wf[n][:, i], w[:, kg, hg]))
            loads += [(wt1_sb[:], wt1), (wt2_sb[:], wt2), (wt3_sb[:], wt3),
                      (bt1_sb[:], bt1), (bt2_sb[:], bt2)]
            for dst, src in loads:
                sp.dma_start(dst, src).then_inc(weights_in, 16)
            assert len(loads) == N_LOADS

            def next_ids(n):
                wait_for, = values(n * (16 * F0) + 16 * F0)
                sp.wait_ge(gathered, wait_for)
                sp.dma_start(ids_sb[:], ids[bass.ds((n + 1) * 128, 128), :]).then_inc(ids_in, 16)

            def result(it):
                sp.wait_ge(side_read, count(sides, it, TOP_DONE))
                sp.dma_start(out[bass.ds(it - 1, 1), :], y_sb[:]).then_inc(y_free, 16)

            def dense(it):
                logits_done, = values(count(sums, it, SUM_STEP[1]))
                sp.wait_ge(summed, logits_done)
                sp.dma_start(logits[1][0:DENSE], dense_t[:, bass.ds((it - 1) * 128, 128)]).then_inc(dense_in, 16)

            def period(n):
                if not isinstance(n, int) or n < BT - 1:
                    next_ids(n)
                for q in range(-1, 3):
                    slot(n, q)
                    if q == 1 and (not isinstance(n, int) or n > 0):
                        dense(n)
                if not isinstance(n, int) or n > 0:
                    result(n)

            sp.wait_ge(pads, 1)
            sp.wait_ge(wl_ready, 1)
            x_to_scratch(0, -1)
            next_ids(0)
            x_replicas(0, -1)
            x_replicas_12(0, -1)
            for q in range(3):
                slot(0, q)
            with sp.Fori(1, BT - 1) as n:
                period(n)
            period(BT - 1)
            slot(BT, -1, False)
            slot(BT, 0, False)
            slot(BT, 1, False)
            dense(BT)
            result(BT)
            sp.wait_ge(y_free, 16 * (BT + 1))

        @block.gpsimd
        def _(pool):
            def lookup(f):
                nc.gpsimd.indirect_dma_start(
                    emb[:, f * D:(f + 1) * D], None, tables[f],
                    bass.IndirectOffsetOnAxis(ids_sb[:, f:f + 1], 0)).then_inc(gathered, 16)

            def low_part(it, j):
                t = absolute(it, j)
                if not (has_chunk(t) and pool_split(j)):
                    return
                n = CHUNKS[j % STEPS][3] - 1
                pool.wait_ge(rounded, count(chunks, it, j))
                nc.gpsimd.tensor_tensor(prod_l[:, j % RING, n], prod[:, j % RING, n],
                                        prod_h[:, j % RING, n].bitcast(FP32), ALU.subtract).then_inc(low_pool, 1)

            def add_up(it, j, layer):
                t = absolute(it, j)
                c = column_of(t, layer)
                if c is None:
                    return
                turn = count(sums, it, j)
                pool.wait_ge(layer_read, turn)
                wait(pool, summed, turn - 1)
                nc.gpsimd.tensor_tensor(half_sum[:].rearrange("p a b -> p (a b)"), r[layer][:, 0:256],
                                        r[layer][:, 256:512], ALU.add).then_inc(halved, 1)
                pool.wait_ge(halved, turn)
                if c % 4 == 0:
                    nc.gpsimd.tensor_tensor(acc[layer][:], half_sum[:, 0], half_sum[:, 1], ALU.add).then_inc(summed, 1)
                    return
                nc.gpsimd.tensor_tensor(dim_sum[:], half_sum[:, 0], half_sum[:, 1], ALU.add).then_inc(quartered, 1)
                pool.wait_ge(quartered, count(later_sums, it, j))
                if c % 4 < 3:
                    ins = nc.gpsimd.tensor_tensor(acc[layer][:], acc[layer][:], dim_sum[:], ALU.add)
                else:
                    wait(pool, side_read, count(sides, it, TOP_DONE - (0 if j > TOP_DONE else PER_IT)))
                    ins = nc.gpsimd.tensor_tensor(logits[layer][:], acc[layer][:], dim_sum[:], ALU.add)
                ins.then_inc(summed, 1)

            def period(it, steps):
                look_up = not isinstance(it, int) or it < BT - 1
                begin = steps[0] if steps[0] < 0 else FIRST[1]
                for j in steps:
                    low_part(it, j)
                    if look_up and begin <= j < LOOKUP_END:
                        i, spread = j - begin, LOOKUP_END - begin
                        if i == 0:
                            pool.wait_ge(ids_in, (it + 2) * 16)
                            pool.wait_ge(emb_moved, it + 1)
                        for f in range(i * F0 // spread, (i + 1) * F0 // spread):
                            lookup(f)
                    for layer in range(3):
                        add_up(it, j - 1, layer)

            pool.wait_ge(ids_in, 16)
            for f in range(F0):
                lookup(f)
            end = PER_IT + PERIOD_START
            period(0, range(end))
            with pool.Fori(1, BT - 1) as it:
                period(it, range(PERIOD_START, end))
            period(BT - 1, range(PERIOD_START, PER_IT))
            period(BT, range(3 * STEPS))

        @block.scalar
        def _(act):
            def move_lookups(n):
                act.wait_ge(gathered, n * (16 * F0))
                nc.scalar.activation(emb_now[:].rearrange("p a f d -> p a (f d)"),
                                     emb[:].unsqueeze(1).to_broadcast([128, 2, F0 * D]), ACT.Copy).then_inc(emb_moved, 1)

            def x_side(it, n, sides_done):
                wait(act, x_out, n * 16)
                act.wait_ge(side_ready, sides_done)
                nc.scalar.activation(x_t[:], side[0:2 * F0, :], ACT.Copy).then_inc(side_read, 1)

            def top_side(it, n, sides_done):
                act.wait_ge(side_ready, sides_done)
                if n == 0:
                    for m in range(U1 // 128):
                        ins = nc.scalar.activation(h1[:, m], side[:, m * 128:(m + 1) * 128], ACT.Relu,
                                                   bias=bt1_sb[:, m:m + 1])
                elif n == 1:
                    for m in range(U2 // 128):
                        ins = nc.scalar.activation(h2[:, m], side[:, m * 128:(m + 1) * 128], ACT.Relu,
                                                   bias=bt2_sb[:, m:m + 1])
                else:
                    act.wait_ge(y_free, it * 16)
                    ins = nc.scalar.activation(y_sb[:], side[0:1, 0:128], ACT.Copy)
                ins.then_inc(side_read, 1)

            def read_layer(it, j, layer):
                t = absolute(it, j)
                c = column_of(t, layer)
                if c is None:
                    return
                act.wait_ge(contracted, count(chunks, it, j - RING - 1))
                wait(act, summed, count(sums, it, j - STEPS))
                if layer < 2:
                    wait(act, xk_out[layer], (it * 4 + (t // STEPS % 4 - layer)) * 16)
                nc.scalar.activation(r[layer][:], z[layer][:], ACT.Relu,
                                     bias=bias[:, layer:layer + 1]).then_inc(layer_read, 1)

            def copy_replica(it, j):
                t = absolute(it, j)
                if not replica(t):
                    return
                layer, first, _, _ = CHUNKS[j % STEPS]
                kg = first // HG
                act.wait_ge(xk_in[kg], count(replicas_of[kg], it, j) * 16)
                wait(act, multiplied, count(chunks, it, j - COPY_AHEAD - 1))
                nc.scalar.activation(rep[:, kg], xk_rep[:, kg], ACT.Copy).then_inc(copied, 1)

            def body(it, steps):
                for j in steps:
                    t = absolute(it, j)
                    g = t // STEPS
                    if j == 3 * STEPS + 1 and (not isinstance(it, int) or it < BT - 1):
                        move_lookups(it + 2)
                    for layer in range(3):
                        read_layer(it, j, layer)
                    copy_replica(it, j + COPY_AHEAD)
                    use = side_use(t - LEAD)
                    if use == "x":
                        x_side(it, it * 4 + (g % 4 + 1), count(sides, it, j - LEAD))
                    elif use is not None:
                        top_side(it, use, count(sides, it, j - LEAD))
                    if has_chunk(t):
                        ns = CHUNKS[j % STEPS][3]
                        act.wait_ge(multiplied, count(chunks, it, j))
                        nc.scalar.activation(prod_h[:, j % RING, 0:ns], prod[:, j % RING, 0:ns],
                                             ACT.Copy).then_inc(rounded, 1)

            act.wait_ge(w0_sum, 1)
            for i, tile in enumerate(SPLIT0):
                ins = nc.scalar.activation(w0h[:, i], stage0a[:, tile], ACT.Copy)
            ins.then_inc(wh_ready, 1)
            act.wait_ge(weights_in, 16 * N_LOADS)
            for n in (1, 2):
                for i, (kg, hg) in enumerate(SPLIT[n]):
                    ins = nc.scalar.activation(wh[n][:, i], stage[n][:, kg, hg], ACT.Copy)
                ins.then_inc(wh_ready, 1)
            move_lookups(1)
            x_side(0, 0, 1)
            each_iteration(act, body)

        @block.vector
        def _(dve):
            def multiply(it, j):
                t = absolute(it, j)
                if not has_chunk(t):
                    return
                g, (layer, first, n, _) = t // STEPS, CHUNKS[j % STEPS]
                dst = prod[:, j % RING, 0:n]
                column = it * 4 + ((g - layer) % 4 + 1 - (4 if g % 4 < layer else 0))
                if layer == 0:
                    dve.wait_ge(rot_in[j % STEPS], column * (16 * (n + (first == 0))))
                elif layer == 1 and first == 0:
                    dve.wait_ge(rep_in, column * (16 * HG))
                if layer == 0:
                    a = x_rep0[:].unsqueeze(1).to_broadcast([128, n, C])
                    b = x_rot[:, first:first + n]
                else:
                    kg, hg = first // HG, first % HG
                    a = x_rep[:, (g - layer) % 4, hg:hg + n]
                    b = rep[:, kg].unsqueeze(1).to_broadcast([128, n, C])
                wait(dve, contracted, count(chunks, it, j - RING))
                if layer:
                    dve.wait_ge(copied, count(replicas, it, j))
                nc.vector.tensor_tensor(dst, a, b, ALU.mult).then_inc(multiplied, 1)

            def low_part(it, j):
                t = absolute(it, j)
                if not has_chunk(t):
                    return
                ns = CHUNKS[j % STEPS][3]
                n = ns - pool_split(j)
                if n == 0:
                    return
                dve.wait_ge(rounded, count(chunks, it, j))
                nc.vector.tensor_tensor(prod_l[:, j % RING, 0:n], prod[:, j % RING, 0:n],
                                        prod_h[:, j % RING, 0:n].bitcast(FP32), ALU.subtract).then_inc(low_dve, 1)

            def body(it, steps):
                for j in steps:
                    multiply(it, j)
                    low_part(it, j - 1)

            for t in (x_rep0[96:128], x_rot[96:128].rearrange("p t c -> p (t c)")):
                ins = nc.vector.memset(t, 0.0)
            ins.then_inc(pads, 1)
            dve.wait_ge(weights_in, 16 * N_LOADS)
            nc.vector.tensor_tensor(stage0a, stage0a, stage0b, ALU.add).then_inc(w0_sum, 1)
            dve.wait_ge(w0_sum, 1)
            dve.wait_ge(wh_ready, 1)
            for i, tile in enumerate(FULL0):
                nc.vector.tensor_copy(w0f[:, i], stage0a[:, tile])
            for i, tile in enumerate(SPLIT0):
                ins = nc.vector.tensor_tensor(w0l[:, i], stage0a[:, tile], w0h[:, i].bitcast(FP32), ALU.subtract)
            ins.then_inc(wl_ready, 1)
            for n in (1, 2):
                dve.wait_ge(wh_ready, n + 1)
                for i, (kg, hg) in enumerate(SPLIT[n]):
                    ins = nc.vector.tensor_tensor(wl[n][:, i], stage[n][:, kg, hg], wh[n][:, i].bitcast(FP32),
                                                  ALU.subtract)
                ins.then_inc(wl_ready, 1)
            dve.wait_ge(wl_ready, 3)
            each_iteration(dve, body)

        @block.tensor
        def _(pe):
            def x_side(g, sides_done):
                wait(pe, side_read, sides_done - 1)
                for i in range(DQ):
                    x = emb_now[:, :, :, g % 4 * DQ + i].rearrange("p a f -> p (a f)")
                    ins = nc.tensor.transpose(side[0:2 * F0, i * 128:(i + 1) * 128], x, ident[:])
                ins.then_inc(side_ready, 1)

            def top_side(it, n, sides_done):
                pe.wait_ge(side_read, sides_done - 1)
                if n == 0:
                    pe.wait_ge(dense_in, it * 16)
                    pe.wait_ge(summed, count(sums, it, 2 * STEPS + SUM_STEP[2]))
                    for m in range(U1 // 128):
                        o, cols = side[:, m * 128:(m + 1) * 128], slice(m * 128, (m + 1) * 128)
                        for n in range(3):
                            ins = nc.tensor.matmul(o, wt1_sb[:, n, cols], logits[n][:], start=(n == 0), stop=(n == 2))
                elif n == 1:
                    for m in range(U2 // 128):
                        for k in range(U1 // 128):
                            ins = nc.tensor.matmul(side[:, m * 128:(m + 1) * 128],
                                                   wt2_sb[:, k, m * 128:(m + 1) * 128], h1[:, k],
                                                   start=(k == 0), stop=(k == U1 // 128 - 1))
                else:
                    for k in range(U2 // 128):
                        ins = nc.tensor.matmul(side[0:1, 0:128], wt3_sb[:, k:k + 1], h2[:, k],
                                               start=(k == 0), stop=(k == U2 // 128 - 1))
                ins.then_inc(side_ready, 1)

            def contract(it, j):
                t = absolute(it, j)
                if not has_chunk(t):
                    return
                layer, first, n, ns = CHUNKS[j % STEPS]
                k, place = j % STEPS, j % RING
                begin, end = k == FIRST[layer], k == LAST[layer]
                acc_z = z[layer][:]
                if begin:
                    wait(pe, layer_read, count(sums, it, j - k + SUM_STEP[layer] - (0 if layer == 2 else STEPS)))
                pe.wait_ge(multiplied, count(chunks, it, j))
                kg, hg = first // HG, first % HG
                for i in range(ns, n):
                    w = w0f[:, FULL0.index(first + i)] if layer == 0 else wf[layer][:, FULL[layer].index((kg, hg + i))]
                    nc.tensor.matmul(acc_z, w, prod[:, place, i], start=begin and i == ns, stop=False)
                begin = begin and n == ns
                pe.wait_ge(rounded, count(chunks, it, j))
                if layer == 0:
                    w_high = [w0h[:, SPLIT0.index(first + i)] for i in range(ns)]
                    w_low = [w0l[:, SPLIT0.index(first + i)] for i in range(ns)]
                else:
                    w_high = [wh[layer][:, SPLIT[layer].index((kg, hg + i))] for i in range(ns)]
                    w_low = [wl[layer][:, SPLIT[layer].index((kg, hg + i))] for i in range(ns)]
                for i in range(ns):
                    nc.tensor.matmul(acc_z, w_high[i], prod_h[:, place, i], start=begin and i == 0, stop=False)
                    nc.tensor.matmul(acc_z, w_low[i], prod_h[:, place, i], start=False, stop=False)
                np_ = pool_split(k)
                if ns > np_:
                    pe.wait_ge(low_dve, count(dve_subs, it, j))
                for i in range(ns):
                    if np_ and i == ns - 1:
                        pe.wait_ge(low_pool, count(pool_subs, it, j))
                    ins = nc.tensor.matmul(acc_z, w_high[i], prod_l[:, place, i], start=False,
                                           stop=end and i == ns - 1)
                ins.then_inc(contracted, 1)

            def body(it, steps):
                for j in steps:
                    t = absolute(it, j)
                    use = side_use(t)
                    if use == "x":
                        if j == 3 * STEPS + X_STEP:
                            pe.wait_ge(emb_moved, it + 2)
                        x_side(t // STEPS + 1, count(sides, it, j))
                    elif use is not None:
                        top_side(it, use, count(sides, it, j))
                    contract(it, j)

            pe.wait_ge(ident_in, 16)
            pe.wait_ge(emb_moved, 1)
            x_side(0, 1)
            pe.wait_ge(weights_in, 16 * N_LOADS)
            pe.wait_ge(wl_ready, 3)
            each_iteration(pe, body)


def kernel(**inputs):
    import numpy as np
    import concourse.bacc as bacc
    from concourse.bass_utils import run_bass_kernel_spmd

    def a(name):
        return np.asarray(inputs[name])

    order0 = np.concatenate([np.arange(HALF, S), np.arange(0, HALF)])
    w0 = a("L0_rec_w0")[:, :, order0]
    w0a = np.zeros((128, NB0, S), w0.dtype)
    w0b = np.zeros((128, NB0, S), w0.dtype)
    for tile in range(NB0):
        for jj in range(3):
            delta = 3 * tile + jj
            for h in range(F0):
                k, p = (h + delta) % F0, 3 * h + jj
                if delta <= F0 // 2:
                    w0a[p, tile] = w0[h, k]
                    if delta:
                        w0b[p, tile] = w0[k, h]
    w12 = []
    for name in ("L0_rec_w1", "L0_rec_w2"):
        w = a(name)
        padded = np.zeros((HG * 8, HALF, S), w.dtype)
        padded[:F0] = w
        w12.append(padded.reshape(HG, 8, KG, 16, S).transpose(3, 1, 2, 0, 4).reshape(128, KG, HG, S))
    wt1 = a("W_top1")
    wt1_layers = np.zeros((128, 3, U1), wt1.dtype)
    wt1_layers[:HALF, 0] = wt1[:HALF]
    wt1_layers[HALF:, 1] = wt1[HALF:S]
    wt1_layers[:, 2] = wt1[S:2 * S]
    wt1_layers[:DENSE, 1] = wt1[2 * S:]
    arrays = {
        "ids": a("ids"),
        "dense_t": a("dense_ctx").T,
        "w0a": w0a, "w0b": w0b, "w1": w12[0], "w2": w12[1],
        "biases": np.stack([a("L0_rec_b0")[order0], a("L0_rec_b1"), a("L0_rec_b2")], axis=1),
        "wt1": wt1_layers,
        "wt2": a("W_top2").reshape(U1 // 128, 128, U2).transpose(1, 0, 2),
        "wt3": a("W_top3")[:, 0].reshape(U2 // 128, 128).T,
        "bt1": a("b_top1").reshape(U1 // 128, 128).T,
        "bt2": a("b_top2").reshape(U2 // 128, 128).T,
        "ident": np.eye(128, dtype=np.float32),
    }
    arrays.update({f"tbl_{f}": a(f"tbl_{f}") for f in range(F0)})
    arrays = {k: np.ascontiguousarray(v) for k, v in arrays.items()}

    nc = bacc.Bacc("TRN2", target_bir_lowering=False, num_devices=1)
    t = {k: nc.dram_tensor(f"in_{k}", v.shape, mybir.dt.from_np(v.dtype), kind="ExternalInput").ap()
         for k, v in arrays.items()}
    out = nc.dram_tensor("out", (BT, 128), FP32, kind="ExternalOutput").ap()
    build(nc, t["ids"], [t[f"tbl_{f}"] for f in range(F0)], t["dense_t"], t["w0a"], t["w0b"], t["w1"], t["w2"],
          t["biases"], t["wt1"], t["wt2"], t["wt3"], t["bt1"], t["bt2"], t["ident"], out)
    r = run_bass_kernel_spmd(nc, [{f"in_{k}": v for k, v in arrays.items()}], core_ids=[0])
    return r.results[0]["out"].reshape(B, 1)
```

```python
from contextlib import ExitStack

import concourse.bass as bass
from concourse import mybir

FP32 = mybir.dt.float32
FP32R = mybir.dt.float32r
I32 = mybir.dt.int32
ALU = mybir.AluOpType
ACT = mybir.ActivationFunctionType

B, F0, D = 2048, 39, 16
S = 128
HALF = S // 2
U1, U2, DENSE = 512, 256, 16
BT = B // 128
DQ = 4
SLOTS = BT * D // DQ
C = DQ * 128
HG, KG = 5, 4
NB0 = 7
STEPS = 20
PER_IT = 4 * STEPS
RING = 5
LEAD = 4
COPY_AHEAD = 2

MORE_SPLIT = ((2, 1),)
SPLIT0, FULL0 = (0, 2, 4, 6), (1, 3, 5)
SPLIT = {n: [(kg, hg) for kg in range(KG) for hg in (0, 1, 3) + ((4,) if (n, kg) in MORE_SPLIT else ())] for n in (1, 2)}
FULL = {n: [(kg, hg) for kg in range(KG) for hg in range(HG) if (kg, hg) not in SPLIT[n]] for n in (1, 2)}
MAX_SPLIT = 2
POOL_RESTS = (2, 6, 10, 14, 18)
CHUNKS = [(0, 0, 2, 1), (0, 2, 2, 1), (0, 4, 2, 1), (0, 6, 1, 1)]
for _layer in (1, 2):
    for _kg in range(KG):
        for _hg, _n in ((0, 3), (3, 2)):
            _split = sum((_kg, hg) in SPLIT[_layer] for hg in range(_hg, _hg + _n))
            CHUNKS.append((_layer, _kg * HG + _hg, _n, _split))
LAST = {0: 3, 1: 11, 2: 19}
FIRST = {0: 0, 1: 4, 2: 12}
SUM_STEP = {0: LAST[0] + RING + 1, 1: LAST[1] + RING + 1, 2: LAST[2] + RING + 1 - STEPS}
TOP_STEPS = (48, 54, 67, 71, 75)
TOP_LOGITS = TOP_STEPS[1]
X_STEPS = (60, 64)
PERIOD_START = X_STEPS[1] + LEAD - PER_IT
LOOKUPS_AT = (3, 5, 7, 8, 10, 12, 13, 14, 15, 17, 19)
ROWS0 = 3 * F0
X_ROWS = F0 + 3 * NB0
X_BLOCKS = -(-F0 * D // 128)
X_REST = F0 * D - 128 * (X_BLOCKS - 1)
X_WRITES = 4


def lookup_steps(period):
    if period == 0:
        begin, end = FIRST[1], 3 * STEPS - 2
        return [begin + f * (end - begin) // F0 for f in range(F0)]
    steps = [slot * STEPS + j for slot in range(-1, 3) for j in LOOKUPS_AT if slot * STEPS + j >= PERIOD_START]
    return steps[:F0]


def pool_split(j):
    return 0 if j % STEPS in POOL_RESTS else 1


def has_chunk(t):
    g, layer = t // STEPS, CHUNKS[t % STEPS][0]
    return t >= 0 and layer <= g < SLOTS + layer


def chunks(t):
    return sum(has_chunk(s) for s in range(t + 1))


def replica(s):
    return has_chunk(s) and CHUNKS[s % STEPS][0] > 0 and CHUNKS[s % STEPS][1] % HG == 0


def replicas(t):
    return sum(replica(s) for s in range(t + 1))


def kg_replicas(t, kg):
    return sum(replica(s) and CHUNKS[s % STEPS][1] // HG == kg for s in range(t + 1))


replicas_of = [lambda t, kg=kg: kg_replicas(t, kg) for kg in range(KG)]


def pool_subs(t):
    return sum(has_chunk(s) and pool_split(s) > 0 for s in range(t + 1))


def dve_subs(t):
    return sum(has_chunk(s) and CHUNKS[s % STEPS][3] > pool_split(s)
               for s in range(t + 1))


def column_of(t, layer):
    g, j = t // STEPS, t % STEPS
    if t < 0 or j != SUM_STEP[layer]:
        return None
    c = g - layer - (1 if layer == 2 else 0)
    return c if 0 <= c < SLOTS else None


def sums(t):
    return sum(column_of(s, layer) is not None for s in range(t + 1) for layer in range(3))


def later_sums(t):
    return sum((column_of(s, layer) or 0) % 4 > 0 for s in range(t + 1) for layer in range(3))


def side_use(t):
    g = t // STEPS
    if t < 0:
        return None
    if g // 4 + 1 < BT and t % PER_IT in X_STEPS:
        return f"x{X_STEPS.index(t % PER_IT)}"
    if g // 4 <= BT and t % PER_IT in TOP_STEPS:
        return TOP_STEPS.index(t % PER_IT)
    return None


def sides(t):
    return 2 + sum(side_use(s) is not None for s in range(t + 1))


N_LOADS = 5 + len(FULL[1]) + len(FULL[2]) + 5

_known = {}


def count(events, it, j):
    def at(n):
        key = (events, n, j)
        if key not in _known:
            _known[key] = events(PER_IT * n + j)
        return _known[key]
    if isinstance(it, int):
        return at(it)
    assert at(1) > 0
    each = at(2) - at(1)
    assert all(at(n) == at(1) + (n - 1) * each for n in range(2, BT - 1))
    return it * each + (at(1) - each)


def wait(engine, sem, value):
    if not isinstance(value, int) or value > 0:
        engine.wait_ge(sem, value)


def build(nc, ids, tables, dense_t, w0a, w0b, w1, w2, biases, wt1, wt2, wt3, bt1, bt2,
          ident_dram, out):
    ctx = ExitStack()
    with ctx:
        def sb(name, shape, dt=FP32):
            return ctx.enter_context(nc.sbuf_tensor(name, shape, dt))

        def sem(name):
            return ctx.enter_context(nc.semaphore(name))

        ids_sb = sb("ids_sb", [128, F0], I32)
        emb = sb("emb", [128, F0 * D])
        x_t = sb("x_t", [128, X_BLOCKS, 128])
        x_rep = sb("x_rep", [128, 4, HG, C])
        x_rep0 = sb("x_rep0", [128, 2, C])
        x_rot = sb("x_rot", [128, NB0, C])
        prod = sb("prod", [128, RING, 3, C])
        prod_h = sb("prod_h", [128, RING, MAX_SPLIT, C], FP32R)
        prod_l = sb("prod_l", [128, RING, MAX_SPLIT, C], FP32R)
        w0h = sb("w0h", [128, len(SPLIT0), S], FP32R)
        w0l = sb("w0l", [128, len(SPLIT0), S], FP32R)
        w0f = sb("w0f", [128, len(FULL0), S])
        wh = {n: sb(f"w{n}h", [128, len(SPLIT[n]), S], FP32R) for n in (1, 2)}
        wl = {n: sb(f"w{n}l", [128, len(SPLIT[n]), S], FP32R) for n in (1, 2)}
        wf = {n: sb(f"w{n}f", [128, len(FULL[n]), S]) for n in (1, 2)}
        ident = sb("ident", [128, 128])
        bias = sb("bias", [128, 3])
        r = {n: sb(f"r{n}", [128, C]) for n in range(3)}
        xk_rep = sb("xk_rep", [128, KG, C])
        half_sum = sb("half_sum", [128, 2, 128])
        dim_sum = sb("dim_sum", [128, 128])
        acc = {n: sb(f"acc{n}", [128, 128]) for n in range(3)}
        logits = {n: sb(f"logits{n}", [128, 128]) for n in range(3)}
        wt1_sb = sb("wt1_sb", [128, 3, U1])
        wt2_sb = sb("wt2_sb", [128, U1 // 128, U2])
        wt3_sb = sb("wt3_sb", [128, U2 // 128])
        bt1_sb = sb("bt1_sb", [128, U1 // 128])
        bt2_sb = sb("bt2_sb", [128, U2 // 128])
        h1 = sb("h1", [128, U1 // 128, 128])
        h2 = sb("h2", [128, U2 // 128, 128])
        y_sb = sb("y_sb", [1, 128])

        z = [ctx.enter_context(nc.psum_tensor(f"z{n}", [128, C], FP32)) for n in range(3)]
        rep = ctx.enter_context(nc.psum_tensor("rep", [128, 4, C], FP32))
        side = ctx.enter_context(nc.psum_tensor("side", [128, C], FP32))

        stage1 = prod[:, 0:2].rearrange("p r t c -> p (r t c)")[:, 0:KG * HG * S]
        stage2 = prod[:, 2:4].rearrange("p r t c -> p (r t c)")[:, 0:KG * HG * S]
        stage = {1: stage1.rearrange("p (k h s) -> p k h s", k=KG, h=HG),
                 2: stage2.rearrange("p (k h s) -> p k h s", k=KG, h=HG)}
        stage0 = x_rep[:, 3].rearrange("p t c -> p (t c)")
        stage0a = stage0[:, 0:NB0 * S].rearrange("p (t s) -> p t s", s=S)
        stage0b = stage0[:, NB0 * S:2 * NB0 * S].rearrange("p (t s) -> p t s", s=S)
        scratch = nc.dram_tensor("scratch", (X_ROWS * D, 128), FP32, kind="Internal").ap()
        scratch_x = scratch.rearrange("(f d) s -> f (d s)", d=D)
        scratch_k = {n: nc.dram_tensor(f"scratch_k{n}", (HALF, C), FP32, kind="Internal").ap() for n in range(2)}

        ident_in = sem("ident_in")
        weights_in = sem("weights_in")
        w0_sum = sem("w0_sum")
        wh_ready = sem("wh_ready")
        wl_ready = sem("wl_ready")
        ids_in = sem("ids_in")
        gathered = sem("gathered")
        x_out = sem("x_out")
        rot_in = [sem(f"rot_in{i}") for i in range(FIRST[1])]
        rep_in = sem("rep_in")
        pads = sem("pads")
        dense_in = sem("dense_in")
        copied = sem("copied")
        multiplied = sem("multiplied")
        rounded = sem("rounded")
        low_dve = sem("low_dve")
        low_pool = sem("low_pool")
        contracted = sem("contracted")
        side_ready = sem("side_ready")
        side_read = sem("side_read")
        layer_read = sem("layer_read")
        xk_out = {n: sem(f"xk_out{n}") for n in range(2)}
        xk_in = [sem(f"xk_in{kg}") for kg in range(KG)]
        summed = sem("summed")
        halved = sem("halved")
        quartered = sem("quartered")
        y_free = sem("y_free")

        block = ctx.enter_context(nc.Block())

        def each_iteration(engine, body):
            body(0, range(PER_IT))
            with engine.Fori(1, BT - 1) as it:
                body(it, range(PER_IT))
            body(BT - 1, range(PER_IT))
            body(BT, range(PER_IT))

        def absolute(it, j):
            return PER_IT * (it if isinstance(it, int) else 1) + j

        @block.sync
        def _(sp):
            def values(*counts):
                return [c if isinstance(c, int) else sp.snap(c) for c in counts]

            def x_to_scratch(it):
                wait(sp, rep_in, it * (4 * 16 * HG))
                sp.wait_ge(side_read, count(sides, it, X_STEPS[1] - PER_IT))
                blocks = scratch[0:128 * (X_BLOCKS - 1)].rearrange("(b p) s -> p b s", p=128)
                sp.dma_start(blocks, x_t[:, 0:X_BLOCKS - 1]).then_inc(x_out, 16)
                sp.dma_start(scratch[128 * (X_BLOCKS - 1):F0 * D], x_t[0:X_REST, X_BLOCKS - 1]).then_inc(x_out, 16)
                twice = scratch[F0 * D:F0 * D + 256].rearrange("(b p) s -> p b s", p=128)
                sp.dma_start(twice, x_t[:, 0:2]).then_inc(x_out, 16)
                sp.dma_start(scratch[F0 * D + 256:X_ROWS * D], x_t[0:(X_ROWS - F0) * D - 256, 2]).then_inc(x_out, 16)

            def x_replicas(it, q):
                cols = slice((q + 1) * C, (q + 2) * C)
                if q == -1:
                    sp.wait_ge(x_out, (it + 1) * (16 * X_WRITES))
                for i, (_, first, n, _) in enumerate(CHUNKS[:FIRST[1]]):
                    wait(sp, multiplied, count(chunks, it, q * STEPS + i))
                    if i == 0:
                        rows = scratch_x[0:F0, cols].unsqueeze(1).to_broadcast([F0, 3, C])
                        sp.dma_start(x_rep0[0:ROWS0, (q + 1) % 2], rows).then_inc(rot_in[0], 16)
                    for t in range(first, first + n):
                        rows = scratch_x[3 * t:3 * t + F0, cols]
                        window = bass.AP(tensor=rows.tensor, offset=rows.offset, ap=[[D * 128, F0], [D * 128, 3], [1, C]])
                        sp.dma_start(x_rot[0:ROWS0, t], window).then_inc(rot_in[i], 16)

            def x_replicas_12(it, q):
                for hg in range(HG):
                    rows = scratch_x[8 * hg:8 * hg + 8, (q + 1) * C:(q + 2) * C].unsqueeze(0).to_broadcast([16, 8, C])
                    sp.dma_start(x_rep[:, (q + 1) % 4, hg], rows).then_inc(rep_in, 16)

            def columns_before(it, q, behind):
                n = it * 4 + (q - behind)
                return None if isinstance(it, int) and not 0 <= n < SLOTS else n

            def xk_to_scratch(it, q, layer):
                if columns_before(it, q, layer) is None:
                    return
                other = q * STEPS + FIRST[2] if layer == 0 else (q + 1) * STEPS + FIRST[1]
                wait(sp, copied, count(replicas, it, other))
                if not replica(absolute(it, other)):
                    sp.wait_ge(layer_read, count(sums, it, q * STEPS + SUM_STEP[layer]))
                half = slice(HALF, S) if layer == 0 else slice(0, HALF)
                sp.dma_start(scratch_k[layer], r[layer][half]).then_inc(xk_out[layer], 16)

            def xk_replica(it, q, layer, kg):
                n = columns_before(it, q, layer + 1)
                if n is None:
                    return
                if kg == 0:
                    sp.wait_ge(xk_out[layer], n * 16 + 16)
                else:
                    before = FIRST[1] if layer == 1 else FIRST[2] - STEPS
                    wait(sp, copied, count(replicas, it, q * STEPS + before + 2 * kg))
                rows = scratch_k[layer][16 * kg:16 * kg + 16].unsqueeze(1).to_broadcast([16, 8, C])
                sp.dma_start(xk_rep[:, kg], rows).then_inc(xk_in[kg], 16)

            def slot(it, q, x=True):
                xk_to_scratch(it, q - 1, 1)
                if x and q == -1:
                    x_to_scratch(it)
                xk_replica(it, q, 1, 0)
                xk_replica(it, q, 1, 1)
                if x:
                    x_replicas(it, q)
                xk_replica(it, q, 1, 2)
                xk_replica(it, q, 1, 3)
                xk_to_scratch(it, q, 0)
                if x:
                    x_replicas_12(it, q)
                for kg in range(KG):
                    xk_replica(it, q + 1, 0, kg)

            sp.dma_start(ids_sb[:], ids[0:128, :]).then_inc(ids_in, 16)
            sp.dma_start(y_sb[:], dense_t[0:1, 0:128]).then_inc(y_free, 16)
            sp.dma_start(ident[:], ident_dram).then_inc(ident_in, 16)
            loads = [(stage0a, w0a), (stage0b, w0b),
                     (stage1, w1.rearrange("p k h s -> p (k h s)")), (stage2, w2.rearrange("p k h s -> p (k h s)")),
                     (bias[:], biases)]
            for n, w in ((1, w1), (2, w2)):
                for i, (kg, hg) in enumerate(FULL[n]):
                    loads.append((wf[n][:, i], w[:, kg, hg]))
            loads += [(wt1_sb[:], wt1), (wt2_sb[:], wt2), (wt3_sb[:], wt3),
                      (bt1_sb[:], bt1), (bt2_sb[:], bt2)]
            for dst, src in loads:
                sp.dma_start(dst, src).then_inc(weights_in, 16)
            assert len(loads) == N_LOADS

            def next_ids(n):
                wait_for, = values(n * (16 * F0) + 16 * F0)
                sp.wait_ge(gathered, wait_for)
                sp.dma_start(ids_sb[:], ids[bass.ds((n + 1) * 128, 128), :]).then_inc(ids_in, 16)

            def dense(it):
                logits_done, = values(count(sums, it, SUM_STEP[1]))
                sp.wait_ge(summed, logits_done)
                sp.dma_start(logits[1][0:DENSE], dense_t[:, bass.ds((it - 1) * 128, 128)]).then_inc(dense_in, 16)

            def period(n):
                if not isinstance(n, int) or n < BT - 1:
                    next_ids(n)
                for q in range(-1, 3):
                    slot(n, q)
                    if q == 1 and (not isinstance(n, int) or n > 0):
                        dense(n)

            sp.wait_ge(pads, 1)
            sp.wait_ge(wl_ready, 1)
            x_to_scratch(0)
            next_ids(0)
            x_replicas(0, -1)
            x_replicas_12(0, -1)
            for q in range(3):
                slot(0, q)
            with sp.Fori(1, BT - 1) as n:
                period(n)
            period(BT - 1)
            slot(BT, -1, False)
            slot(BT, 0, False)
            slot(BT, 1, False)
            dense(BT)
            sp.wait_ge(y_free, 16 * (BT + 1))

        @block.gpsimd
        def _(pool):
            def lookup(f):
                nc.gpsimd.indirect_dma_start(
                    emb[:, f * D:(f + 1) * D], None, tables[f],
                    bass.IndirectOffsetOnAxis(ids_sb[:, f:f + 1], 0)).then_inc(gathered, 16)

            def low_part(it, j):
                t = absolute(it, j)
                if not (has_chunk(t) and pool_split(j)):
                    return
                n = CHUNKS[j % STEPS][3] - 1
                pool.wait_ge(rounded, count(chunks, it, j))
                nc.gpsimd.tensor_tensor(prod_l[:, j % RING, n], prod[:, j % RING, n],
                                        prod_h[:, j % RING, n].bitcast(FP32), ALU.subtract).then_inc(low_pool, 1)

            def add_up(it, j, layer):
                t = absolute(it, j)
                c = column_of(t, layer)
                if c is None:
                    return
                turn = count(sums, it, j)
                pool.wait_ge(layer_read, turn)
                wait(pool, summed, turn - 1)
                nc.gpsimd.tensor_tensor(half_sum[:].rearrange("p a b -> p (a b)"), r[layer][:, 0:256],
                                        r[layer][:, 256:512], ALU.add).then_inc(halved, 1)
                pool.wait_ge(halved, turn)
                if c % 4 == 0:
                    nc.gpsimd.tensor_tensor(acc[layer][:], half_sum[:, 0], half_sum[:, 1], ALU.add).then_inc(summed, 1)
                    return
                nc.gpsimd.tensor_tensor(dim_sum[:], half_sum[:, 0], half_sum[:, 1], ALU.add).then_inc(quartered, 1)
                pool.wait_ge(quartered, count(later_sums, it, j))
                if c % 4 < 3:
                    ins = nc.gpsimd.tensor_tensor(acc[layer][:], acc[layer][:], dim_sum[:], ALU.add)
                else:
                    wait(pool, side_read, count(sides, it, TOP_LOGITS - (0 if j > TOP_LOGITS else PER_IT)))
                    ins = nc.gpsimd.tensor_tensor(logits[layer][:], acc[layer][:], dim_sum[:], ALU.add)
                ins.then_inc(summed, 1)

            def period(it, steps):
                last = isinstance(it, int) and it >= BT - 1
                lookups = [] if last else lookup_steps(it if isinstance(it, int) else 1)
                for j in steps:
                    if lookups and j == lookups[0]:
                        pool.wait_ge(ids_in, (it + 2) * 16)
                        pool.wait_ge(side_ready, count(sides, it, X_STEPS[1] - PER_IT))
                    low_part(it, j)
                    for f in [f for f, step in enumerate(lookups) if step == j]:
                        lookup(f)
                    for layer in range(3):
                        add_up(it, j - 1, layer)

            pool.wait_ge(ids_in, 16)
            for f in range(F0):
                lookup(f)
            end = PER_IT + PERIOD_START
            period(0, range(end))
            with pool.Fori(1, BT - 1) as it:
                period(it, range(PERIOD_START, end))
            period(BT - 1, range(PERIOD_START, PER_IT))
            period(BT, range(3 * STEPS))

        @block.scalar
        def _(act):
            def x_side(it, part, sides_done):
                wait(act, x_out, it * (16 * X_WRITES))
                act.wait_ge(side_ready, sides_done)
                if part == 0:
                    ins = nc.scalar.activation(x_t[:, 0:X_BLOCKS - 1].rearrange("p b s -> p (b s)"), side[:], ACT.Copy)
                else:
                    ins = nc.scalar.activation(x_t[0:X_REST, X_BLOCKS - 1], side[0:X_REST, 0:128], ACT.Copy)
                ins.then_inc(side_read, 1)

            def top_side(it, n, sides_done):
                act.wait_ge(side_ready, sides_done)
                if isinstance(it, int) and it == 0:
                    act.nop().then_inc(side_read, 1)
                    return
                if n < 2:
                    for m in (2 * n, 2 * n + 1):
                        ins = nc.scalar.activation(h1[:, m], side[:, m * 128:(m + 1) * 128], ACT.Relu,
                                                   bias=bt1_sb[:, m:m + 1])
                elif n < 4:
                    m = n - 2
                    ins = nc.scalar.activation(h2[:, m], side[:, m * 128:(m + 1) * 128], ACT.Relu,
                                               bias=bt2_sb[:, m:m + 1])
                else:
                    act.wait_ge(y_free, it * 16)
                    ins = nc.scalar.activation(y_sb[:], side[0:1, 0:128], ACT.Copy)
                ins.then_inc(side_read, 1)
                if n == 4:
                    act.wait_ge(side_read, sides_done)
                    nc.scalar.dma_start(out[bass.ds(it - 1, 1), :], y_sb[:]).then_inc(y_free, 16)

            def read_layer(it, j, layer):
                t = absolute(it, j)
                c = column_of(t, layer)
                if c is None:
                    return
                act.wait_ge(contracted, count(chunks, it, j - RING - 1))
                wait(act, summed, count(sums, it, j - STEPS))
                if layer < 2:
                    wait(act, xk_out[layer], (it * 4 + (t // STEPS % 4 - layer)) * 16)
                nc.scalar.activation(r[layer][:], z[layer][:], ACT.Relu,
                                     bias=bias[:, layer:layer + 1]).then_inc(layer_read, 1)

            def copy_replica(it, j):
                t = absolute(it, j)
                if not replica(t):
                    return
                layer, first, _, _ = CHUNKS[j % STEPS]
                kg = first // HG
                act.wait_ge(xk_in[kg], count(replicas_of[kg], it, j) * 16)
                wait(act, multiplied, count(chunks, it, j - COPY_AHEAD - 1))
                nc.scalar.activation(rep[:, kg], xk_rep[:, kg], ACT.Copy).then_inc(copied, 1)

            def body(it, steps):
                for j in steps:
                    t = absolute(it, j)
                    for layer in range(3):
                        read_layer(it, j, layer)
                    copy_replica(it, j + COPY_AHEAD)
                    use = side_use(t - LEAD)
                    if use in ("x0", "x1"):
                        x_side(it + 1, int(use[1]), count(sides, it, j - LEAD))
                    elif use is not None:
                        top_side(it, use, count(sides, it, j - LEAD))
                    if has_chunk(t):
                        ns = CHUNKS[j % STEPS][3]
                        act.wait_ge(multiplied, count(chunks, it, j))
                        nc.scalar.activation(prod_h[:, j % RING, 0:ns], prod[:, j % RING, 0:ns],
                                             ACT.Copy).then_inc(rounded, 1)

            act.wait_ge(w0_sum, 1)
            for i, tile in enumerate(SPLIT0):
                ins = nc.scalar.activation(w0h[:, i], stage0a[:, tile], ACT.Copy)
            ins.then_inc(wh_ready, 1)
            act.wait_ge(weights_in, 16 * N_LOADS)
            for n in (1, 2):
                for i, (kg, hg) in enumerate(SPLIT[n]):
                    ins = nc.scalar.activation(wh[n][:, i], stage[n][:, kg, hg], ACT.Copy)
                ins.then_inc(wh_ready, 1)
            x_side(0, 0, 1)
            x_side(0, 1, 2)
            each_iteration(act, body)

        @block.vector
        def _(dve):
            def multiply(it, j):
                t = absolute(it, j)
                if not has_chunk(t):
                    return
                g, (layer, first, n, _) = t // STEPS, CHUNKS[j % STEPS]
                dst = prod[:, j % RING, 0:n]
                column = it * 4 + ((g - layer) % 4 + 1 - (4 if g % 4 < layer else 0))
                if layer == 0:
                    dve.wait_ge(rot_in[j % STEPS], column * (16 * (n + (first == 0))))
                elif layer == 1 and first == 0:
                    dve.wait_ge(rep_in, column * (16 * HG))
                if layer == 0:
                    a = x_rep0[:, g % 2].unsqueeze(1).to_broadcast([128, n, C])
                    b = x_rot[:, first:first + n]
                else:
                    kg, hg = first // HG, first % HG
                    a = x_rep[:, (g - layer) % 4, hg:hg + n]
                    b = rep[:, kg].unsqueeze(1).to_broadcast([128, n, C])
                wait(dve, contracted, count(chunks, it, j - RING))
                if layer:
                    dve.wait_ge(copied, count(replicas, it, j))
                nc.vector.tensor_tensor(dst, a, b, ALU.mult).then_inc(multiplied, 1)

            def low_part(it, j):
                t = absolute(it, j)
                if not has_chunk(t):
                    return
                ns = CHUNKS[j % STEPS][3]
                n = ns - pool_split(j)
                if n == 0:
                    return
                dve.wait_ge(rounded, count(chunks, it, j))
                nc.vector.tensor_tensor(prod_l[:, j % RING, 0:n], prod[:, j % RING, 0:n],
                                        prod_h[:, j % RING, 0:n].bitcast(FP32), ALU.subtract).then_inc(low_dve, 1)

            def body(it, steps):
                for j in steps:
                    multiply(it, j)
                    low_part(it, j - 1)

            for t in (x_rep0[96:128].rearrange("p t c -> p (t c)"), x_rot[96:128].rearrange("p t c -> p (t c)")):
                ins = nc.vector.memset(t, 0.0)
            ins.then_inc(pads, 1)
            dve.wait_ge(weights_in, 16 * N_LOADS)
            nc.vector.tensor_tensor(stage0a, stage0a, stage0b, ALU.add).then_inc(w0_sum, 1)
            dve.wait_ge(w0_sum, 1)
            dve.wait_ge(wh_ready, 1)
            for i, tile in enumerate(FULL0):
                nc.vector.tensor_copy(w0f[:, i], stage0a[:, tile])
            for i, tile in enumerate(SPLIT0):
                ins = nc.vector.tensor_tensor(w0l[:, i], stage0a[:, tile], w0h[:, i].bitcast(FP32), ALU.subtract)
            ins.then_inc(wl_ready, 1)
            for n in (1, 2):
                dve.wait_ge(wh_ready, n + 1)
                for i, (kg, hg) in enumerate(SPLIT[n]):
                    ins = nc.vector.tensor_tensor(wl[n][:, i], stage[n][:, kg, hg], wh[n][:, i].bitcast(FP32),
                                                  ALU.subtract)
                ins.then_inc(wl_ready, 1)
            dve.wait_ge(wl_ready, 3)
            each_iteration(dve, body)

        @block.tensor
        def _(pe):
            def x_side(it, part, sides_done):
                wait(pe, side_read, sides_done - 1)
                if part == 0:
                    pe.wait_ge(gathered, (it + 1) * (16 * F0))
                for b in range(X_BLOCKS - 1) if part == 0 else [X_BLOCKS - 1]:
                    rows = min(128, F0 * D - b * 128)
                    col = b * 128 if part == 0 else 0
                    ins = nc.tensor.transpose(side[0:rows, col:col + 128], emb[:, b * 128:b * 128 + rows], ident[:])
                ins.then_inc(side_ready, 1)

            def top_side(it, n, sides_done):
                pe.wait_ge(side_read, sides_done - 1)
                if isinstance(it, int) and it == 0:
                    pe.nop().then_inc(side_ready, 1)
                    return
                if n == 0:
                    pe.wait_ge(dense_in, it * 16)
                    pe.wait_ge(summed, count(sums, it, 2 * STEPS + SUM_STEP[2]))
                if n < 2:
                    for m in (2 * n, 2 * n + 1):
                        cols = slice(m * 128, (m + 1) * 128)
                        for layer in range(3):
                            ins = nc.tensor.matmul(side[:, cols], wt1_sb[:, layer, cols], logits[layer][:],
                                                   start=(layer == 0), stop=(layer == 2))
                elif n < 4:
                    cols = slice((n - 2) * 128, (n - 1) * 128)
                    for k in range(U1 // 128):
                        ins = nc.tensor.matmul(side[:, cols], wt2_sb[:, k, cols], h1[:, k],
                                               start=(k == 0), stop=(k == U1 // 128 - 1))
                else:
                    for k in range(U2 // 128):
                        ins = nc.tensor.matmul(side[0:1, 0:128], wt3_sb[:, k:k + 1], h2[:, k],
                                               start=(k == 0), stop=(k == U2 // 128 - 1))
                ins.then_inc(side_ready, 1)

            def contract(it, j):
                t = absolute(it, j)
                if not has_chunk(t):
                    return
                layer, first, n, ns = CHUNKS[j % STEPS]
                k, place = j % STEPS, j % RING
                begin, end = k == FIRST[layer], k == LAST[layer]
                acc_z = z[layer][:]
                if begin:
                    wait(pe, layer_read, count(sums, it, j - k + SUM_STEP[layer] - (0 if layer == 2 else STEPS)))
                pe.wait_ge(multiplied, count(chunks, it, j))
                kg, hg = first // HG, first % HG
                for i in range(ns, n):
                    w = w0f[:, FULL0.index(first + i)] if layer == 0 else wf[layer][:, FULL[layer].index((kg, hg + i))]
                    nc.tensor.matmul(acc_z, w, prod[:, place, i], start=begin and i == ns, stop=False)
                begin = begin and n == ns
                pe.wait_ge(rounded, count(chunks, it, j))
                if layer == 0:
                    w_high = [w0h[:, SPLIT0.index(first + i)] for i in range(ns)]
                    w_low = [w0l[:, SPLIT0.index(first + i)] for i in range(ns)]
                else:
                    w_high = [wh[layer][:, SPLIT[layer].index((kg, hg + i))] for i in range(ns)]
                    w_low = [wl[layer][:, SPLIT[layer].index((kg, hg + i))] for i in range(ns)]
                for i in range(ns):
                    nc.tensor.matmul(acc_z, w_high[i], prod_h[:, place, i], start=begin and i == 0, stop=False)
                    nc.tensor.matmul(acc_z, w_low[i], prod_h[:, place, i], start=False, stop=False)
                np_ = pool_split(k)
                if ns > np_:
                    pe.wait_ge(low_dve, count(dve_subs, it, j))
                for i in range(ns):
                    if np_ and i == ns - 1:
                        pe.wait_ge(low_pool, count(pool_subs, it, j))
                    ins = nc.tensor.matmul(acc_z, w_high[i], prod_l[:, place, i], start=False,
                                           stop=end and i == ns - 1)
                ins.then_inc(contracted, 1)

            def body(it, steps):
                for j in steps:
                    t = absolute(it, j)
                    use = side_use(t)
                    if use in ("x0", "x1"):
                        x_side(it + 1, int(use[1]), count(sides, it, j))
                    elif use is not None:
                        top_side(it, use, count(sides, it, j))
                    contract(it, j)

            pe.wait_ge(ident_in, 16)
            x_side(0, 0, 1)
            x_side(0, 1, 2)
            pe.wait_ge(weights_in, 16 * N_LOADS)
            pe.wait_ge(wl_ready, 3)
            each_iteration(pe, body)


def kernel(**inputs):
    import numpy as np
    import concourse.bacc as bacc
    from concourse.bass_utils import run_bass_kernel_spmd

    def a(name):
        return np.asarray(inputs[name])

    order0 = np.concatenate([np.arange(HALF, S), np.arange(0, HALF)])
    w0 = a("L0_rec_w0")[:, :, order0]
    w0a = np.zeros((128, NB0, S), w0.dtype)
    w0b = np.zeros((128, NB0, S), w0.dtype)
    for tile in range(NB0):
        for jj in range(3):
            delta = 3 * tile + jj
            for h in range(F0):
                k, p = (h + delta) % F0, 3 * h + jj
                if delta <= F0 // 2:
                    w0a[p, tile] = w0[h, k]
                    if delta:
                        w0b[p, tile] = w0[k, h]
    w12 = []
    for name in ("L0_rec_w1", "L0_rec_w2"):
        w = a(name)
        padded = np.zeros((HG * 8, HALF, S), w.dtype)
        padded[:F0] = w
        w12.append(padded.reshape(HG, 8, KG, 16, S).transpose(3, 1, 2, 0, 4).reshape(128, KG, HG, S))
    wt1 = a("W_top1")
    wt1_layers = np.zeros((128, 3, U1), wt1.dtype)
    wt1_layers[:HALF, 0] = wt1[:HALF]
    wt1_layers[HALF:, 1] = wt1[HALF:S]
    wt1_layers[:, 2] = wt1[S:2 * S]
    wt1_layers[:DENSE, 1] = wt1[2 * S:]
    arrays = {
        "ids": a("ids"),
        "dense_t": a("dense_ctx").T,
        "w0a": w0a, "w0b": w0b, "w1": w12[0], "w2": w12[1],
        "biases": np.stack([a("L0_rec_b0")[order0], a("L0_rec_b1"), a("L0_rec_b2")], axis=1),
        "wt1": wt1_layers,
        "wt2": a("W_top2").reshape(U1 // 128, 128, U2).transpose(1, 0, 2),
        "wt3": a("W_top3")[:, 0].reshape(U2 // 128, 128).T,
        "bt1": a("b_top1").reshape(U1 // 128, 128).T,
        "bt2": a("b_top2").reshape(U2 // 128, 128).T,
        "ident": np.eye(128, dtype=np.float32),
    }
    arrays.update({f"tbl_{f}": a(f"tbl_{f}") for f in range(F0)})
    arrays = {k: np.ascontiguousarray(v) for k, v in arrays.items()}

    nc = bacc.Bacc("TRN2", target_bir_lowering=False, num_devices=1)
    t = {k: nc.dram_tensor(f"in_{k}", v.shape, mybir.dt.from_np(v.dtype), kind="ExternalInput").ap()
         for k, v in arrays.items()}
    out = nc.dram_tensor("out", (BT, 128), FP32, kind="ExternalOutput").ap()
    build(nc, t["ids"], [t[f"tbl_{f}"] for f in range(F0)], t["dense_t"], t["w0a"], t["w0b"], t["w1"], t["w2"],
          t["biases"], t["wt1"], t["wt2"], t["wt3"], t["bt1"], t["bt2"], t["ident"], out)
    r = run_bass_kernel_spmd(nc, [{f"in_{k}": v for k, v in arrays.items()}], core_ids=[0])
    return r.results[0]["out"].reshape(B, 1)
```
